# Optimizing a Trainium2 kernel written in Bass

```python
import numpy as np
import jax
import jax.numpy as jnp

def _softmax(x, axis=-1):
    return jax.nn.softmax(x, axis=axis)

def _gelu(x):
    return jax.nn.gelu(x, approximate=True)

def _silu(x):
    return jax.nn.silu(x)

def _sigmoid(x):
    return jax.nn.sigmoid(x)

def _layernorm(x, axis=-1, eps=1e-05):
    m = jnp.mean(x, axis=axis, keepdims=True)
    v = jnp.var(x, axis=axis, keepdims=True)
    return (x - m) / jnp.sqrt(v + eps)

def _scatter_add(tgt, idx, src, axis=0):
    return tgt.at[idx].add(src)

def _segment_sum(src, seg, n):
    return jax.ops.segment_sum(src, seg, n)
kernel_name = 'mk_gnn_ffn_d1_gnn_r32_7790d2'

def setup_inputs(seed: int=0):
    np.random.seed(seed)
    _w = jnp.asarray

    def _rec_inputs():
        import jax
        import jax.numpy as jnp
        _gk = jax.random.key(seed)
        x = -0.000202 + 1 * jax.random.normal(jax.random.fold_in(_gk, 1), (3125, 256), jnp.float32)
        src = jax.random.randint(jax.random.fold_in(_gk, 2), (50000,), 0, 3125, jnp.int32)
        dst = jax.random.randint(jax.random.fold_in(_gk, 3), (50000,), 0, 3125, jnp.int32)
        _o = jnp.argsort(dst, stable=True)
        src = src[_o]
        dst = dst[_o]
        edge_attr_4 = 0.00121237 + 1.00026 * jax.random.normal(jax.random.fold_in(_gk, 12), (50000, 4), jnp.float32)
        edge_attr_8 = jax.random.uniform(jax.random.fold_in(_gk, 13), (50000, 8), jnp.float32, 0.0, 1)
        node_vec1 = jax.random.uniform(jax.random.fold_in(_gk, 14), (3125, 1), jnp.float32, 0.0, 1)
        return (x, src, dst, edge_attr_4, edge_attr_8, node_vec1)
    x, src, dst, edge_attr_4, edge_attr_8, node_vec1 = _rec_inputs()

    def _L0_gnn_setup():
        import jax, jax.numpy as jnp
        import numpy as np
        N = 25000
        E = 12500
        MUL = 64
        NB = 8
        RN = 64
        NUM_NEIGH = 16.0
        INV_SQRT3 = 1.0 / np.sqrt(3.0)

        def _forward(node_input, node_attr, edge_attr, edge_length_embedded, W_sc0, W_sc1, W_lin1_0, W_lin1_1, fc_w0, fc_w1, W_lin2_0, W_lin2_1, edge_src, edge_dst):
            Nn = node_input.shape[0]
            z = node_attr
            x0 = node_input[:, :MUL]
            x1 = node_input[:, MUL:].reshape(Nn, MUL, 3)
            inv_m = 1.0 / np.sqrt(MUL)
            s0 = x0 @ W_sc0 * z * inv_m
            s1 = jnp.einsum('nuc,uv->nvc', x1, W_sc1) * z[:, :, None] * inv_m
            h0 = x0 @ W_lin1_0 * z * inv_m
            h1 = jnp.einsum('nuc,uv->nvc', x1, W_lin1_1) * z[:, :, None] * inv_m
            hid = jax.nn.silu(edge_length_embedded @ fc_w0 / np.sqrt(NB))
            w = hid @ fc_w1 / np.sqrt(RN)
            wA, wB, wC, wD = (w[:, :MUL], w[:, MUL:2 * MUL], w[:, 2 * MUL:3 * MUL], w[:, 3 * MUL:])
            xs0 = h0[edge_src]
            xs1 = h1[edge_src]
            sh0 = edge_attr[:, :1]
            sh1 = edge_attr[:, 1:4]
            midA = wA * xs0 * sh0
            midD = wD * jnp.einsum('euc,ec->eu', xs1, sh1) * INV_SQRT3
            midB = (wB * xs0)[:, :, None] * sh1[:, None, :]
            midC = wC[:, :, None] * xs1 * sh0[:, None, :]
            mid0 = jnp.concatenate([midA, midD], axis=1)
            mid1 = jnp.concatenate([midB, midC], axis=1)
            inv_nb = 1.0 / np.sqrt(NUM_NEIGH)
            y0 = jax.ops.segment_sum(mid0, edge_dst, num_segments=Nn) * inv_nb
            y1 = jax.ops.segment_sum(mid1.reshape(mid1.shape[0], -1), edge_dst, num_segments=Nn).reshape(Nn, 2 * MUL, 3) * inv_nb
            inv_2m = 1.0 / np.sqrt(2 * MUL)
            o0 = y0 @ W_lin2_0 * z * inv_2m
            o1 = jnp.einsum('nuc,uv->nvc', y1, W_lin2_1) * z[:, :, None] * inv_2m
            c_s = np.float32(np.sin(np.pi / 8.0))
            c_x = np.float32(np.cos(np.pi / 8.0))
            out0 = c_s * s0 + c_x * o0
            out1 = c_s * s1 + c_x * o1
            return jnp.concatenate([out0, out1.reshape(Nn, 3 * MUL)], axis=1)
        key = jax.random.key(seed)
        ks = jax.random.split(key, 14)
        f32 = jnp.float32
        return {'node_input': jax.random.normal(ks[0], (N, 4 * MUL), f32), 'node_attr': jnp.ones((N, 1), f32), 'edge_src': jax.random.randint(ks[1], (E,), 0, N, dtype=jnp.int32), 'edge_dst': jax.random.randint(ks[2], (E,), 0, N, dtype=jnp.int32), 'edge_attr': jax.random.normal(ks[3], (E, 4), f32), 'edge_length_embedded': jax.random.uniform(ks[4], (E, NB), f32), 'W_sc0': jax.random.normal(ks[5], (MUL, MUL), f32), 'W_sc1': jax.random.normal(ks[6], (MUL, MUL), f32), 'W_lin1_0': jax.random.normal(ks[7], (MUL, MUL), f32), 'W_lin1_1': jax.random.normal(ks[8], (MUL, MUL), f32), 'fc_w0': jax.random.normal(ks[9], (NB, RN), f32), 'fc_w1': jax.random.normal(ks[10], (RN, 4 * MUL), f32), 'W_lin2_0': jax.random.normal(ks[11], (2 * MUL, MUL), f32), 'W_lin2_1': jax.random.normal(ks[12], (2 * MUL, MUL), f32)}
    _L0_gnn_all = _L0_gnn_setup()
    _L0_gnn_in = {k: v for k, v in _L0_gnn_all.items() if k in ('W_sc0', 'W_sc1', 'W_lin1_0', 'W_lin1_1', 'fc_w0', 'fc_w1', 'W_lin2_0', 'W_lin2_1')}
    del _L0_gnn_all

    def _L0_ffn_setup():
        import jax, jax.numpy as jnp
        import numpy as np
        B, S, D, F, E, K = (8, 64, 256, 1024, 8, 2)
        key = jax.random.key(seed)
        ks = jax.random.split(key, 10)
        s = 0.02
        return {'x': jax.random.normal(ks[0], (B, S, D), dtype=jnp.float32), 'Wr': jax.random.normal(ks[1], (D, E), dtype=jnp.float32) * s, 'W1s': jax.random.normal(ks[2], (D, F), dtype=jnp.float32) * s, 'b1s': jnp.zeros((F,), dtype=jnp.float32), 'W2s': jax.random.normal(ks[3], (F, D), dtype=jnp.float32) * s, 'b2s': jnp.zeros((D,), dtype=jnp.float32), 'W1p': jax.random.normal(ks[4], (E, D, F), dtype=jnp.float32) * s, 'b1p': jnp.zeros((E, F), dtype=jnp.float32), 'W2p': jax.random.normal(ks[5], (E, F, D), dtype=jnp.float32) * s, 'b2p': jnp.zeros((E, D), dtype=jnp.float32)}
    _L0_ffn_all = _L0_ffn_setup()
    _L0_ffn_in = {k: v for k, v in _L0_ffn_all.items() if k in ('Wr', 'W1s', 'b1s', 'W2s', 'b2s', 'W1p', 'b1p', 'W2p', 'b2p')}
    del _L0_ffn_all
    return {'x': x, 'src': src, 'dst': dst, 'edge_attr_4': edge_attr_4, 'edge_attr_8': edge_attr_8, 'node_vec1': node_vec1, 'L0_gnn_W_sc0': _L0_gnn_in['W_sc0'], 'L0_gnn_W_sc1': _L0_gnn_in['W_sc1'], 'L0_gnn_W_lin1_0': _L0_gnn_in['W_lin1_0'], 'L0_gnn_W_lin1_1': _L0_gnn_in['W_lin1_1'], 'L0_gnn_fc_w0': _L0_gnn_in['fc_w0'], 'L0_gnn_fc_w1': _L0_gnn_in['fc_w1'], 'L0_gnn_W_lin2_0': _L0_gnn_in['W_lin2_0'], 'L0_gnn_W_lin2_1': _L0_gnn_in['W_lin2_1'], 'L0_ffn_Wr': _L0_ffn_in['Wr'], 'L0_ffn_W1s': _L0_ffn_in['W1s'], 'L0_ffn_b1s': _L0_ffn_in['b1s'], 'L0_ffn_W2s': _L0_ffn_in['W2s'], 'L0_ffn_b2s': _L0_ffn_in['b2s'], 'L0_ffn_W1p': _L0_ffn_in['W1p'], 'L0_ffn_b1p': _L0_ffn_in['b1p'], 'L0_ffn_W2p': _L0_ffn_in['W2p'], 'L0_ffn_b2p': _L0_ffn_in['b2p']}

def reference(x, src, dst, edge_attr_4, edge_attr_8, node_vec1, L0_gnn_W_sc0, L0_gnn_W_sc1, L0_gnn_W_lin1_0, L0_gnn_W_lin1_1, L0_gnn_fc_w0, L0_gnn_fc_w1, L0_gnn_W_lin2_0, L0_gnn_W_lin2_1, L0_ffn_Wr, L0_ffn_W1s, L0_ffn_b1s, L0_ffn_W2s, L0_ffn_b2s, L0_ffn_W1p, L0_ffn_b1p, L0_ffn_W2p, L0_ffn_b2p):
    import jax
    import jax.numpy as jnp

    def _L0_gnn_ref(node_input, node_attr, edge_src, edge_dst, edge_attr, edge_length_embedded, W_sc0, W_sc1, W_lin1_0, W_lin1_1, fc_w0, fc_w1, W_lin2_0, W_lin2_1):
        import jax, jax.numpy as jnp
        import numpy as np
        N = 25000
        E = 12500
        MUL = 64
        NB = 8
        RN = 64
        NUM_NEIGH = 16.0
        INV_SQRT3 = 1.0 / np.sqrt(3.0)

        def _forward(node_input, node_attr, edge_attr, edge_length_embedded, W_sc0, W_sc1, W_lin1_0, W_lin1_1, fc_w0, fc_w1, W_lin2_0, W_lin2_1, edge_src, edge_dst):
            Nn = node_input.shape[0]
            z = node_attr
            x0 = node_input[:, :MUL]
            x1 = node_input[:, MUL:].reshape(Nn, MUL, 3)
            inv_m = 1.0 / np.sqrt(MUL)
            s0 = x0 @ W_sc0 * z * inv_m
            s1 = jnp.einsum('nuc,uv->nvc', x1, W_sc1) * z[:, :, None] * inv_m
            h0 = x0 @ W_lin1_0 * z * inv_m
            h1 = jnp.einsum('nuc,uv->nvc', x1, W_lin1_1) * z[:, :, None] * inv_m
            hid = jax.nn.silu(edge_length_embedded @ fc_w0 / np.sqrt(NB))
            w = hid @ fc_w1 / np.sqrt(RN)
            wA, wB, wC, wD = (w[:, :MUL], w[:, MUL:2 * MUL], w[:, 2 * MUL:3 * MUL], w[:, 3 * MUL:])
            xs0 = h0[edge_src]
            xs1 = h1[edge_src]
            sh0 = edge_attr[:, :1]
            sh1 = edge_attr[:, 1:4]
            midA = wA * xs0 * sh0
            midD = wD * jnp.einsum('euc,ec->eu', xs1, sh1) * INV_SQRT3
            midB = (wB * xs0)[:, :, None] * sh1[:, None, :]
            midC = wC[:, :, None] * xs1 * sh0[:, None, :]
            mid0 = jnp.concatenate([midA, midD], axis=1)
            mid1 = jnp.concatenate([midB, midC], axis=1)
            inv_nb = 1.0 / np.sqrt(NUM_NEIGH)
            y0 = jax.ops.segment_sum(mid0, edge_dst, num_segments=Nn) * inv_nb
            y1 = jax.ops.segment_sum(mid1.reshape(mid1.shape[0], -1), edge_dst, num_segments=Nn).reshape(Nn, 2 * MUL, 3) * inv_nb
            inv_2m = 1.0 / np.sqrt(2 * MUL)
            o0 = y0 @ W_lin2_0 * z * inv_2m
            o1 = jnp.einsum('nuc,uv->nvc', y1, W_lin2_1) * z[:, :, None] * inv_2m
            c_s = np.float32(np.sin(np.pi / 8.0))
            c_x = np.float32(np.cos(np.pi / 8.0))
            out0 = c_s * s0 + c_x * o0
            out1 = c_s * s1 + c_x * o1
            return jnp.concatenate([out0, out1.reshape(Nn, 3 * MUL)], axis=1)
        return _forward(node_input, node_attr, edge_attr, edge_length_embedded, W_sc0, W_sc1, W_lin1_0, W_lin1_1, fc_w0, fc_w1, W_lin2_0, W_lin2_1, edge_src, edge_dst)

    def _L0_ffn_ref(x, Wr, W1s, b1s, W2s, b2s, W1p, b1p, W2p, b2p):
        import jax, jax.numpy as jnp
        import numpy as np
        B, S, D, F, E, K = (8, 64, 256, 1024, 8, 2)
        gelu = lambda t: jax.nn.gelu(t, approximate=False)
        shared = gelu(x @ W1s + b1s) @ W2s + b2s
        rw = jax.nn.softmax(x @ Wr, axis=-1)
        topw, topi = jax.lax.top_k(rw, K)
        topw = topw / jnp.sum(topw, axis=-1, keepdims=True)
        mask = jnp.sum(jax.nn.one_hot(topi, E, dtype=topw.dtype) * topw[..., None], axis=-2)
        h = gelu(jnp.einsum('bsd,edf->bsef', x, W1p) + b1p)
        priv = jnp.einsum('bsef,efd->bsed', h, W2p) + b2p
        routed = jnp.einsum('bsed,bse->bsd', priv, mask)
        return shared + routed
    x = x + _L0_gnn_ref(_layernorm(x, axis=-1), node_vec1, src, dst, edge_attr_4, edge_attr_8, L0_gnn_W_sc0, L0_gnn_W_sc1, L0_gnn_W_lin1_0, L0_gnn_W_lin1_1, L0_gnn_fc_w0, L0_gnn_fc_w1, L0_gnn_W_lin2_0, L0_gnn_W_lin2_1)
    x = x + _L0_ffn_ref(_layernorm(x, axis=-1)[None], L0_ffn_Wr, L0_ffn_W1s, L0_ffn_b1s, L0_ffn_W2s, L0_ffn_b2s, L0_ffn_W1p, L0_ffn_b1p, L0_ffn_W2p, L0_ffn_b2p)[0]
    return x

_drawn_inputs = setup_inputs


def setup_inputs(seed=0):
    import zlib

    import numpy as np

    out = dict(_drawn_inputs(seed))
    spreads = {'L0_ffn_b1s': (0.0, 0.1),
     'L0_ffn_b2s': (0.0, 0.1),
     'L0_ffn_b1p': (0.0, 0.337),
     'L0_ffn_b2p': (0.0, 0.1)}
    factors = {}
    for name, (base, spread) in spreads.items():
        noise = np.random.default_rng([zlib.crc32(name.encode()), seed]).standard_normal(out[name].shape)
        drawn = base * np.exp(spread * noise) if base else spread * noise
        out[name] = jnp.asarray(drawn.astype(out[name].dtype))
    for name, factor in factors.items():
        out[name] = (out[name] * factor).astype(out[name].dtype)
    return out
```

```python
from contextlib import ExitStack

import numpy as np

import concourse.bass as bass
from concourse import mybir

ALU = mybir.AluOpType
ACT = mybir.ActivationFunctionType
F32 = mybir.dt.float32
F32R = mybir.dt.float32r
I32 = mybir.dt.int32
AX_X = mybir.AxisListType.X

P = 128
NODES, FEAT, EDGES = 3125, 256, 50000
MUL, NB, RN, NUM_NEIGH = 64, 8, 64, 16.0
HID, EXPERTS = 1024, 8
EPS = 1e-5

NT = -(-NODES // P)
NPAD = NT * P
GROUP = 5
NG = NT // GROUP
C = 4
STEP = C * P
T = -(-EDGES // STEP)
EPAD = T * STEP
HALF = P // 2
TOK = 256
SUB = TOK // P
TILES = (2 * NPAD + EXPERTS * TOK) // TOK
SLOTS = (TILES + 1) * TOK
ROW = FEAT + 2
KC = FEAT // P
FC = HID // P
SH = GROUP * P
SHH = SH // 2
assert NG * GROUP == NT and T % 2 == 0

C_S = float(np.float32(np.sin(np.pi / 8.0)))
C_X = float(np.float32(np.cos(np.pi / 8.0)))
INV_M = 1.0 / float(np.sqrt(MUL))
OUT_SCALE = C_X / float(np.sqrt(2 * MUL)) / float(np.sqrt(NUM_NEIGH))
INV_SQRT3 = 1.0 / float(np.sqrt(3.0))


def at(i, n=1):
    return bass.ds(i, n)


def gnn_moe_kernel(nc, x, src_t, dst_t, dst_w, sh_t, ele_t, z_t, w_sc0, w_sc1, w_l0, w_l1, fc0, fc1, w_20, w_21,
                   w_r, w1, b1, w2, b2, out):
    def dram(name, shape, dt=F32):
        return nc.dram_tensor(name, shape, dt, kind="Internal").ap()

    h_tab = dram("h_tab", (NPAD, FEAT))
    ele_split = dram("ele_split", (2 * NB, EPAD))
    span_d = dram("span_d", (T, 2))
    xnew_d = dram("xnew_d", (NPAD, FEAT))
    xn_d = dram("xn_d", (NPAD, FEAT))
    xT_d = dram("xT_d", (2, P, KC, NPAD))
    slots_d = dram("slots_d", (SLOTS, ROW))

    with ExitStack() as whole:
        def keep(name, shape, dt=F32):
            return whole.enter_context(nc.sbuf_tensor(name, shape, dt))

        ident = keep("ident", [P, P])
        ones = keep("ones", [P, P])
        earlier = keep("earlier", [P, P])
        iota_row = keep("iota_row", [P, P])
        counts_i = keep("counts_i", [1, 2 * EXPERTS], I32)
        pos_i = keep("pos_i", [P, NT, 2], I32)
        meta_i = keep("meta_i", [P, NT, 2, 2], I32)
        logits = keep("logits", [P, NT, EXPERTS])

        with ExitStack() as graph:
            def gkeep(name, shape, dt=F32):
                return graph.enter_context(nc.sbuf_tensor(name, shape, dt))

            x_sb = gkeep("x_sb", [P, NT, FEAT])
            s_sb = gkeep("s_sb", [P, NT, FEAT])
            y_sb = gkeep("y_sb", [P, NT + 1, 8, MUL])
            zo = gkeep("zo", [P, NT])
            rounds_i = gkeep("rounds_i", [1, 1], I32)
            first_block = gkeep("first_block", [P, T])
            node_block(nc, locals())
            edge_block(nc, locals())
            update_block(nc, locals())
        route_block(nc, locals())
        expert_blocks(nc, locals())


def chain_of(eng, sem):
    done = [0]

    def link(ins):
        done[0] += 1
        ins.then_inc(sem, 1)
        eng.wait_ge(sem, done[0])

    return link


def node_block(nc, v):
    x, z_t, dst_w, ele_t = v["x"], v["z_t"], v["dst_w"], v["ele_t"]
    x_sb, s_sb, zo = v["x_sb"], v["s_sb"], v["zo"]
    ident, ones, earlier, iota_row = v["ident"], v["ones"], v["earlier"], v["iota_row"]
    h_tab, ele_split, span_d = v["h_tab"], v["ele_split"], v["span_d"]
    first_block, rounds_i, y_sb, out = v["first_block"], v["rounds_i"], v["y_sb"], v["out"]
    EW = NB * EPAD // P

    with ExitStack() as ctx:
        def sb(name, shape, dt=F32):
            return ctx.enter_context(nc.sbuf_tensor(name, shape, dt))

        def pb(name):
            return ctx.enter_context(nc.psum_tensor(name, [P, 512], F32))

        def sem(name):
            return ctx.enter_context(nc.semaphore(name))

        z_sb = sb("z_sb", [P, NT])
        zi = sb("zi", [P, NT])
        zs = sb("zs", [P, NT])
        wpair = sb("wpair", [P, 2, 4 * MUL])
        stats = sb("stats", [P, NT, 6])
        mv = sb("mv", [P, NT, 2])
        root = sb("root", [P, NT])
        rstd = sb("rstd", [P, NT])
        eps = sb("eps", [P, 1])
        xn = sb("xn", [P, GROUP, FEAT])
        xT = sb("xT", [P, 2, FEAT])
        h_rows = sb("h_rows", [P, GROUP, FEAT])
        dst_i = sb("dst_i", [T, STEP], I32)
        dst_f = sb("dst_f", [T, STEP])
        span = sb("span", [T, 2])
        span_all = sb("span_all", [P, T, 2])
        low_i = sb("low_i", [P, T], I32)
        far = sb("far", [P, T])
        far_i = sb("far_i", [P, T], I32)
        far_f = sb("far_f", [P, T])
        rounds = sb("rounds", [P, 1])
        e_raw = sb("e_raw", [P, EW])
        e_hi = sb("e_hi", [P, EW], F32R)
        e_lo = sb("e_lo", [P, EW], F32R)
        psT = [pb(f"node_psT{i}") for i in range(2)]
        psH = [pb(f"node_psH{i}") for i in range(2)]

        z_in, w_in, dst_in, e_in, x_in = sem("z_in"), sem("w_in"), sem("dst_in"), sem("e_in"), sem("x_in")
        span_out, span_in, e_out, h_out = sem("span_out"), sem("span_in"), sem("e_out"), sem("h_out")
        consts, wzero, zscaled = sem("consts"), sem("wzero"), sem("zscaled")
        pool_step, dve_step = sem("pool_step"), sem("dve_step")
        e_split_hi, e_split_lo, span_done = sem("e_split_hi"), sem("e_split_lo"), sem("span_done")
        passed = sem("passed")
        x_ready, stats_done, aggr_done, root_done = sem("x_ready"), sem("stats_done"), sem("aggr_done"), sem("root_done")
        xn_ready, turned, xT_ready = sem("xn_ready"), sem("turned"), sem("xT_ready")
        mixed, h_ready, s_ready = sem("mixed"), sem("h_ready"), sem("s_ready")
        block = ctx.enter_context(nc.Block())

        @block.sync
        def _(sp):
            sp.dma_start(z_sb[:], z_t).then_inc(z_in, 16)
            with sp.Fori(0, NG) as g:
                sp.dma_start(x_sb[:, at(g * GROUP, GROUP), :],
                             x.rearrange("(t p) f -> p t f", p=P)[:, at(g * GROUP, GROUP), :]).then_inc(x_in, 16)
                sp.wait_ge(x_in, 16 * (g + 1))
                sp.sem_inc(x_ready, 1)
            sp.wait_ge(span_done, 1)
            sp.dma_start(span_d, span[:]).then_inc(span_out, 16)
            sp.wait_ge(span_out, 16)
            sp.dma_start(span_all[:], span_d.rearrange("t (o c) -> o t c", o=1).to_broadcast([P, T, 2])
                         ).then_inc(span_in, 16)
            flat = ele_split.rearrange("r e -> (r e)").rearrange("(h p w) -> h p w", h=2, p=P)
            sp.wait_ge(e_split_hi, 1)
            sp.dma_start(flat[0], e_hi[:].bitcast(F32)).then_inc(e_out, 16)
            sp.wait_ge(e_split_lo, 1)
            sp.dma_start(flat[1], e_lo[:].bitcast(F32)).then_inc(e_out, 16)
            sp.wait_ge(e_out, 32)

        @block.gpsimd
        def _(pool):
            link = chain_of(pool, pool_step)
            link(pool.memset(wpair[:], 0.0))
            pool.sem_inc(wzero, 1)
            link(pool.memset(eps[:], EPS))
            link(pool.memset(ident[:], 0.0))
            link(pool.affine_select(out=ident[:], in_=ident[:], compare_op=ALU.not_equal, fill=1.0, base=0,
                                    pattern=[[-1, P]], channel_multiplier=1))
            link(pool.memset(ones[:], 1.0))
            link(pool.affine_select(out=earlier[:], in_=ones[:], compare_op=ALU.is_ge, fill=0.0, base=-1,
                                    pattern=[[1, P]], channel_multiplier=-1))
            link(pool.iota(iota_row[:], [[1, P]], base=0, channel_multiplier=0,
                           allow_small_or_imprecise_dtypes=True))
            link(pool.memset(y_sb[:], 0.0))
            pool.sem_inc(consts, 1)

        @block.vector
        def _(dve):
            link = chain_of(dve, dve_step)
            dve.wait_ge(z_in, 16)
            nc.vector.tensor_scalar(zi[:], z_sb[:], INV_M, None, ALU.mult)
            nc.vector.tensor_scalar(zs[:], z_sb[:], INV_M * C_S, None, ALU.mult)
            nc.vector.tensor_scalar(zo[:], z_sb[:], OUT_SCALE, None, ALU.mult).then_inc(zscaled, 1)
            with dve.Fori(0, NG) as g:
                dve.wait_ge(x_ready, g + 1)
                dve.sem_inc(passed, 1)
                for j in range(GROUP):
                    ins = nc.vector.bn_stats(stats[:, at(g * GROUP + j), :], x_sb[:, at(g * GROUP + j), :])
                ins.then_inc(stats_done, 1)
            dve.wait_ge(stats_done, NG)
            for t in range(NT):
                ins = nc.vector.bn_aggr(mv[:, t, :], stats[:, t, :])
            ins.then_inc(aggr_done, 1)
            dve.wait_ge(root_done, 1)
            link(nc.vector.reciprocal(rstd[:], root[:]))
            with dve.Fori(0, NG) as g:
                for j in range(GROUP):
                    dve.wait_ge(turned, g * GROUP + j + 1)
                    row = x_sb[:, at(g * GROUP + j), :].rearrange("p o f -> p (o f)")
                    mean = mv[:, at(g * GROUP + j), 0:1].rearrange("p o c -> p (o c)")
                    scale = rstd[:, at(g * GROUP + j)]
                    nc.vector.tensor_scalar(xn[:, j, 0:MUL], row[:, 0:MUL], mean, scale,
                                            ALU.subtract, ALU.mult)
                    nc.vector.tensor_scalar(xn[:, j, MUL:].rearrange("p (c u) -> p u c", c=3),
                                            row[:, MUL:].rearrange("p (u c) -> p u c", c=3),
                                            mean, scale,
                                            ALU.subtract, ALU.mult).then_inc(xn_ready, 1)
            dve.wait_ge(dst_in, 16)
            link(nc.vector.tensor_copy(dst_f[:], dst_i[:]))
            nc.vector.tensor_reduce(span[:, 0:1], dst_f[:], AX_X, ALU.min)
            nc.vector.tensor_reduce(span[:, 1:2], dst_f[:], AX_X, ALU.max).then_inc(span_done, 1)
            dve.wait_ge(e_split_hi, 1)
            nc.vector.tensor_tensor(e_lo[:], e_raw[:], e_hi[:].bitcast(F32), ALU.subtract).then_inc(e_split_lo, 1)
            dve.wait_ge(span_in, 16)
            link(nc.vector.tensor_copy(low_i[:], span_all[:, :, 0]))
            link(nc.vector.tensor_single_scalar(low_i[:], low_i[:], 6, ALU.logical_shift_right))
            link(nc.vector.tensor_copy(first_block[:], low_i[:]))
            link(nc.vector.scalar_tensor_tensor(out=far[:], in0=first_block[:], scalar=-float(HALF),
                                                in1=span_all[:, :, 1], op0=ALU.mult, op1=ALU.add))
            link(nc.vector.tensor_copy(far_i[:], far[:]))
            link(nc.vector.tensor_single_scalar(far_i[:], far_i[:], 7, ALU.logical_shift_right))
            link(nc.vector.tensor_copy(far_f[:], far_i[:]))
            link(nc.vector.tensor_reduce(rounds[:], far_f[:], AX_X, ALU.max))
            link(nc.vector.tensor_scalar(rounds[:], rounds[:], 1.0, None, ALU.add))
            link(nc.vector.tensor_copy(rounds_i[:], rounds[0:1, :]))

        @block.scalar
        def _(act):
            act.wait_ge(wzero, 1)
            act.wait_ge(pool_step, 1)
            w_l0, w_l1, w_sc0, w_sc1 = v["w_l0"], v["w_l1"], v["w_sc0"], v["w_sc1"]
            for pair in range(2):
                for half, (lin, own) in enumerate([(w_l0, w_sc0), (w_l1, w_sc1)] if pair == 0
                                                  else [(w_l1, w_sc1)] * 2):
                    rows = slice(MUL * half, MUL * half + MUL)
                    act.dma_start(wpair[rows, pair, MUL * half:MUL * half + MUL], lin).then_inc(w_in, 16)
                    act.dma_start(wpair[rows, pair, 2 * MUL + MUL * half:3 * MUL + MUL * half], own
                                  ).then_inc(w_in, 16)
            act.dma_start(dst_i[:], dst_w).then_inc(dst_in, 16)
            act.dma_start(e_raw[:], ele_t.rearrange("b e -> (b e)").rearrange("(p w) -> p w", p=P)).then_inc(e_in, 16)
            act.wait_ge(zscaled, 1)
            act.wait_ge(pool_step, 2)
            act.wait_ge(aggr_done, 1)
            nc.scalar.activation(root[:], mv[:, :, 1], ACT.Sqrt, bias=eps[:]).then_inc(root_done, 1)
            act.sem_inc(xT_ready, 1)
            act.sem_inc(s_ready, 1)
            with act.Fori(0, NG) as g:
                for j in range(GROUP):
                    b = j % 2
                    t = g * GROUP + j
                    act.wait_ge(turned, t + 1 + GROUP)
                    act.wait_ge(mixed, t + 1 + (1 if j == 0 else 0))
                    nc.scalar.activation(xT[:, b, :], psT[b][:, 0:FEAT], ACT.Copy).then_inc(xT_ready, 1)
                    act.wait_ge(mixed, t + 1 + 2)
                    if j == 0:
                        act.wait_ge(h_out, 16 * (g + 1))
                    pair = psH[b][:, :].rearrange("p (a k w) -> p a k w", a=2, k=2)
                    nc.scalar.activation(h_rows[:, j, :].rearrange("p (a w) -> p a w", a=2), pair[:, :, 0, :],
                                         ACT.Copy, scale=zi[:, at(t)]).then_inc(h_ready, 1)
                    nc.scalar.activation(s_sb[:, at(t), :].rearrange("p o (a w) -> p (o a) w", a=2), pair[:, :, 1, :],
                                         ACT.Copy, scale=zs[:, at(t)]).then_inc(s_ready, 1)
                act.wait_ge(h_ready, (g + 1) * GROUP)
                act.dma_start(h_tab.rearrange("(t p) f -> p t f", p=P)[:, at(g * GROUP, GROUP), :], h_rows[:]
                              ).then_inc(h_out, 16)
            act.wait_ge(e_in, 16)
            nc.scalar.activation(e_hi[:], e_raw[:], ACT.Copy).then_inc(e_split_hi, 1)
            act.wait_ge(h_out, 16 * (NG + 1))

        @block.tensor
        def _(pe):
            pe.wait_ge(consts, 1)
            pe.wait_ge(pool_step, 8)
            pe.wait_ge(w_in, 16 * 8)
            pe.sem_inc(turned, GROUP)
            pe.sem_inc(mixed, 2)
            pe.sem_inc(h_out, 16)
            with pe.Fori(0, NG) as g:
                def turn(j):
                    t = g * GROUP + j
                    pe.wait_ge(xn_ready, t + 1)
                    pe.wait_ge(xT_ready, t + 1 if j == 0 else t)
                    for a in range(2):
                        ins = nc.tensor.transpose(psT[j % 2][:, P * a:P * a + P], xn[:, j, P * a:P * a + P], ident[:])
                    ins.then_inc(turned, 1)

                def mix(j):
                    t = g * GROUP + j
                    pe.wait_ge(xT_ready, t + 2)
                    pe.wait_ge(s_ready, t + 1 if j == 0 else t)
                    for a in range(2):
                        ins = nc.tensor.matmul(psH[j % 2][:, 4 * MUL * a:4 * MUL * (a + 1)],
                                               xT[:, j % 2, P * a:P * a + P], wpair[:, a, :], start=True, stop=True)
                    ins.then_inc(mixed, 1)

                turn(0)
                for j in range(GROUP):
                    if j + 1 < GROUP:
                        turn(j + 1)
                    mix(j)


def edge_block(nc, v):
    dst_t, src_t, sh_t, fc0, fc1 = v["dst_t"], v["src_t"], v["sh_t"], v["fc0"], v["fc1"]
    iota_row, first_block, rounds_i, y_sb = v["iota_row"], v["first_block"], v["rounds_i"], v["y_sb"]
    h_tab, ele_split, slots_d, out = v["h_tab"], v["ele_split"], v["slots_d"], v["out"]

    with ExitStack() as ctx:
        def sb(name, shape, dt=F32):
            return ctx.enter_context(nc.sbuf_tensor(name, shape, dt))

        def pb(name):
            return ctx.enter_context(nc.psum_tensor(name, [P, 512], F32))

        def sem(name):
            return ctx.enter_context(nc.semaphore(name))

        src_sb = sb("src_sb", [P, T, C], I32)
        dst_ti = sb("dst_ti", [P, T, C], I32)
        dst_all = sb("dst_all", [P, T, C])
        residue_i = sb("residue_i", [P, T, C], I32)
        residue = sb("residue", [P, T, C])
        key = sb("key", [P, T, C])
        outside = sb("outside", [P, T, C])
        sh_sb = sb("sh_sb", [P, T, 4 * C])
        window = sb("window", [P, T])
        row_t = sb("row_t", [1, T])
        low_row = sb("low_row", [1, T], I32)
        high_row = sb("high_row", [1, T], I32)
        w0raw = sb("w0raw", [MUL, P])
        w0hi = sb("w0hi", [MUL, P], F32R)
        w0 = sb("w0", [MUL, P], F32R)
        w1raw = sb("w1raw", [P, 4 * MUL])
        w1hi = sb("w1hi", [P, 4 * MUL], F32R)
        w1lo = sb("w1lo", [P, 4 * MUL], F32R)
        e_st = [sb(f"e_st{i}", [MUL, STEP], F32R) for i in range(2)]
        src_st = [sb(f"src_st{i}", [P, C], I32) for i in range(2)]
        sh_st = [sb(f"sh_st{i}", [P, 4 * C]) for i in range(2)]
        hid = [sb(f"hid{i}", [P, STEP]) for i in range(2)]
        hidT = [sb(f"hidT{i}", [P, STEP], F32R) for i in range(2)]
        rows = [sb(f"rows{i}", [P, C, 4, MUL]) for i in range(2)]
        prod = [sb(f"prod{i}", [P, C, 8 * MUL]) for i in range(2)]
        hot = [sb(f"hot{i}", [P, C, P]) for i in range(2)]
        hots = [sb(f"hots{i}", [P, 4 * C, P]) for i in range(2)]
        blank = sb("blank", [P, ROW])
        psE = pb("psE")
        psW = [[pb(f"psW{i}{k}") for k in range(2)] for i in range(2)]
        psY = [pb(f"psY{i}") for i in range(2)]

        tab_in, w_in, z_out = sem("tab_in"), sem("ew_in"), sem("z_out")
        dve_step, pool_step, blank_set = sem("edve_step"), sem("epool_step"), sem("blank_set")
        weights_ready = sem("weights_ready")
        e_in = [sem(f"ee_in{i}") for i in range(2)]
        row_in = [[sem(f"row_in{i}{c}") for c in range(C)] for i in range(2)]
        hid_done, silu_done, round_done, low_done = sem("hid_done"), sem("silu_done"), sem("round_done"), sem("low_done")
        w_done, prod_done, hot_done, sh_staged = sem("w_done"), sem("prod_done"), sem("hot_done"), sem("sh_staged")
        hots_done, seg_done, y_done, src_staged = sem("hots_done"), sem("seg_done"), sem("y_done"), sem("src_staged")
        gather_turn = sem("gather_turn")
        block = ctx.enter_context(nc.Block())


        @block.sync
        def _(sp):
            for dst, src in ((src_sb, src_t), (dst_ti, dst_t)):
                sp.dma_start(dst[:].rearrange("p t c -> p (t c)"), src).then_inc(tab_in, 16)
            sp.dma_start(sh_sb[:].rearrange("p t c -> p (t c)"), sh_t).then_inc(tab_in, 16)
            sp.wait_ge(blank_set, 1)
            sp.dma_start(slots_d.rearrange("(n p) f -> p n f", p=P),
                         blank[:].unsqueeze(1).to_broadcast([P, SLOTS // P, ROW])).then_inc(z_out, 16)
            sp.dma_start(out[NPAD:NPAD + P, :], blank[:, 0:FEAT]).then_inc(z_out, 16)
            sp.wait_ge(weights_ready, 1)
            R = sp.value_load(rounds_i[0:1, 0:1], min_val=1, max_val=NPAD // P)
            with sp.Fori(0, R) as r:
                with sp.Fori(0, T // 2) as k:
                    for p in range(2):
                        t = k * 2 + p
                        first_edge = sp.snap(t * STEP)
                        sp.wait_ge(hid_done, r * T + t + 1)
                        for half in range(2):
                            sp.dma_start(e_st[p][32 * half:32 * half + 2 * NB, :].bitcast(F32),
                                         ele_split[:, at(first_edge, STEP)]).then_inc(e_in[p], 16)
            sp.wait_ge(z_out, 32)

        @block.gpsimd
        def _(pool):
            link = chain_of(pool, pool_step)
            link(pool.memset(blank[:], 0.0))
            link(pool.iota(blank[:, FEAT:FEAT + 1].bitcast(I32), [[0, 1]], base=NPAD, channel_multiplier=1))
            pool.sem_inc(blank_set, 1)
            pool.wait_ge(tab_in, 48)
            pool.wait_ge(weights_ready, 1)
            R = pool.value_load(rounds_i[0:1, 0:1], min_val=1, max_val=NPAD // P)
            with pool.Fori(0, R) as r:
                with pool.Fori(0, T // 2) as k:
                    for p in range(2):
                        t = k * 2 + p
                        pool.wait_ge(prod_done, (r * T + t) * C + C)
                        pool.tensor_copy(src_st[p][:], src_sb[:, at(t), :].rearrange("p o c -> p (o c)")
                                         ).then_inc(src_staged, 1)
                        pool.wait_ge(src_staged, r * T + t + 1)
                        pool.sem_inc(gather_turn, 1)
                        for c in range(C):
                            pool.indirect_dma_start(
                                out=rows[p][:, c, :, :].rearrange("p a u -> p (a u)"), out_offset=None, in_=h_tab,
                                in_offset=bass.IndirectOffsetOnAxis(ap=src_st[p][:, c:c + 1], axis=0),
                            ).then_inc(row_in[p][c], 16)

        @block.scalar
        def _(act):
            act.wait_ge(dve_step, 1)
            for half in range(2):
                act.dma_start(w0raw[32 * half:32 * half + 2 * NB, :], fc0).then_inc(w_in, 16)
            act.dma_start(w1raw[:], fc1).then_inc(w_in, 16)
            act.wait_ge(weights_ready, 1)
            act.wait_ge(tab_in, 48)
            R = act.value_load(rounds_i[0:1, 0:1], min_val=1, max_val=NPAD // P)

            def silu(r, j, p):
                act.wait_ge(hid_done, r * T + j + 1 + 2)
                act.wait_ge(low_done, r * T + j + 1)
                nc.scalar.activation(hid[p][:], psE[:], ACT.Silu, scale=1.0 / float(np.sqrt(NB))).then_inc(silu_done, 1)
                act.wait_ge(silu_done, r * T + j + 1 + 1)
                act.wait_ge(w_done, r * T + j + 1)
                nc.scalar.activation(hidT[p][:], hid[p][:], ACT.Copy).then_inc(round_done, 1)

            def scale_hot(r, j, p):
                act.wait_ge(hots_done, r * T + j + 1)
                nc.scalar.activation(sh_st[p][:], sh_sb[:, at(j), :].rearrange("p o c -> p (o c)"),
                                     ACT.Copy).then_inc(sh_staged, 1)
                act.wait_ge(sh_staged, r * T + j + 1)
                act.wait_ge(hot_done, r * T + j + 1)
                act.wait_ge(seg_done, r * T + j + 1)
                for c in range(C):
                    for k in range(4):
                        ins = nc.scalar.activation(hots[p][:, 4 * c + k, :], hot[p][:, c, :], ACT.Copy,
                                                   scale=sh_st[p][:, 4 * c + k:4 * c + k + 1])
                ins.then_inc(hots_done, 1)

            act.sem_inc(silu_done, 1)
            act.sem_inc(hots_done, 2)
            with act.Fori(0, R) as r:
                silu(r, 0, 0)
                silu(r, 1, 1)
                scale_hot(r, 0, 0)
                with act.Fori(0, T // 2 - 1) as k:
                    for p in range(2):
                        silu(r, k * 2 + p + 2, p)
                        scale_hot(r, k * 2 + p + 1, 1 - p)
                scale_hot(r, T - 1, 1)

        @block.vector
        def _(dve):
            link = chain_of(dve, dve_step)
            for t in e_st:
                nc.vector.memset(t[:].bitcast(F32), 0.0)
            link(nc.vector.memset(w0raw[:], 0.0))
            dve.wait_ge(w_in, 16 * 3)
            link(nc.vector.tensor_copy(w0hi[:], w0raw[:]))
            nc.vector.tensor_copy(w0[0:32, :], w0raw[0:32, :])
            link(nc.vector.tensor_tensor(w0[32:64, :], w0raw[32:64, :], w0hi[32:64, :].bitcast(F32), ALU.subtract))
            link(nc.vector.tensor_scalar(w1raw[:], w1raw[:], 1.0 / float(np.sqrt(RN)), None, ALU.mult))
            link(nc.vector.tensor_copy(w1hi[:], w1raw[:]))
            link(nc.vector.tensor_tensor(w1lo[:], w1raw[:], w1hi[:].bitcast(F32), ALU.subtract))
            dve.wait_ge(tab_in, 48)
            link(nc.vector.tensor_copy(dst_all[:], dst_ti[:]))
            link(nc.vector.tensor_single_scalar(residue_i[:], dst_ti[:], P - 1, ALU.bitwise_and))
            link(nc.vector.tensor_copy(residue[:], residue_i[:]))
            link(nc.vector.tensor_copy(window[:], first_block[:]))
            dve.sem_inc(weights_ready, 1)
            setup_links = 10
            dve.sem_inc(low_done, 2)
            dve.sem_inc(prod_done, 2 * C)
            dve.sem_inc(y_done, 2)
            R = dve.value_load(rounds_i[0:1, 0:1], min_val=1, max_val=NPAD // P)

            def one_hot(r, j, p):
                dve.wait_ge(hots_done, r * T + j + 1)
                nc.vector.tensor_tensor(hot[p][:], iota_row[:].unsqueeze(1).to_broadcast([P, C, P]),
                                        key[:, at(j), :].rearrange("p o c -> p (o c)").unsqueeze(2).to_broadcast([P, C, P]),
                                        ALU.is_equal).then_inc(hot_done, 1)

            def low(r, j, p):
                dve.wait_ge(round_done, r * T + j + 1)
                nc.vector.tensor_tensor(hidT[p][MUL:P, :], hid[p][MUL:P, :], hidT[p][MUL:P, :].bitcast(F32),
                                        ALU.subtract).then_inc(low_done, 1)

            def products(r, k, j, p):
                dve.wait_ge(w_done, r * T + j + 1 + 2)
                dve.wait_ge(seg_done, r * T + j + 1)
                for c in range(C):
                    dve.wait_ge(row_in[p][c], 16 * (r * (T // 2) + k + 1))
                    w = psW[p][c // 2][:, 256 * (c % 2):256 * (c % 2) + 256].rearrange("p (a u) -> p a u", u=MUL)
                    slots = prod[p][:, c, :].rearrange("p (a u) -> p a u", u=MUL)
                    nc.vector.tensor_tensor(slots[:, 0::7, :], w[:, 0:2, :],
                                            rows[p][:, c, 0:1, :].to_broadcast([P, 2, MUL]), ALU.mult)
                    nc.vector.tensor_tensor(
                        slots[:, 1:7, :].rearrange("p (b k) u -> p b k u", b=2),
                        w[:, 2:4, :].unsqueeze(2).to_broadcast([P, 2, 3, MUL]),
                        rows[p][:, c, 1:4, :].unsqueeze(1).to_broadcast([P, 2, 3, MUL]), ALU.mult
                    ).then_inc(prod_done, 1)

            def add_y(r, j, p):
                low_tile = dve.value_load(low_row[0:1, at(j)], min_val=0, max_val=NT)
                high_tile = dve.value_load(high_row[0:1, at(j)], min_val=0, max_val=NT)
                dve.wait_ge(seg_done, r * T + j + 1 + 2)
                dve.wait_ge(y_done, r * T + j + 2)
                for lo, tile in ((0, low_tile), (HALF, high_tile)):
                    acc = y_sb[lo:lo + HALF, at(tile), :, :].rearrange("p o a u -> p (o a u)")
                    ins = nc.vector.tensor_tensor(acc, acc, psY[p][lo:lo + HALF, :], ALU.add)
                ins.then_inc(y_done, 1)

            with dve.Fori(0, R) as r:
                base = setup_links + r * 12
                n = [0]

                def step(ins):
                    n[0] += 1
                    ins.then_inc(dve_step, 1)
                    dve.wait_ge(dve_step, base + n[0])

                wb = window[:].unsqueeze(2).to_broadcast([P, T, C])
                step(nc.vector.scalar_tensor_tensor(out=key[:], in0=wb, scalar=-float(HALF), in1=dst_all[:],
                                                    op0=ALU.mult, op1=ALU.add))
                step(nc.vector.tensor_scalar(outside[:], key[:], 0.0, 1000.0, ALU.is_lt, ALU.mult))
                step(nc.vector.tensor_scalar(key[:], key[:], float(P), 1000.0, ALU.is_ge, ALU.mult))
                step(nc.vector.tensor_tensor(key[:], key[:], outside[:], ALU.add))
                step(nc.vector.tensor_tensor(key[:], key[:], residue[:], ALU.add))
                step(nc.vector.tensor_scalar(row_t[:], window[0:1, :], 1.0, 2.0 * NT, ALU.add, ALU.min))
                step(nc.vector.tensor_copy(low_row[:], row_t[:]))
                step(nc.vector.tensor_single_scalar(low_row[:], low_row[:], 1, ALU.logical_shift_right))
                step(nc.vector.tensor_scalar(row_t[:], window[0:1, :], 2.0 * NT, None, ALU.min))
                step(nc.vector.tensor_copy(high_row[:], row_t[:]))
                step(nc.vector.tensor_single_scalar(high_row[:], high_row[:], 1, ALU.logical_shift_right))
                step(nc.vector.tensor_scalar(window[:], window[:], 2.0, None, ALU.add))
                one_hot(r, 0, 0)
                low(r, 0, 0)
                one_hot(r, 1, 1)
                low(r, 1, 1)
                products(r, 0, 0, 0)
                one_hot(r, 2, 0)
                low(r, 2, 0)
                products(r, 0, 1, 1)
                with dve.Fori(0, T // 2 - 2) as k:
                    for q in range(2):
                        t = k * 2 + 1 + q
                        add_y(r, t - 1, q)
                        one_hot(r, t + 2, 1 - q)
                        low(r, t + 2, 1 - q)
                        products(r, k + 1, t + 1, q)
                add_y(r, T - 4, 0)
                one_hot(r, T - 1, 1)
                low(r, T - 1, 1)
                products(r, T // 2 - 1, T - 2, 0)
                add_y(r, T - 3, 1)
                products(r, T // 2 - 1, T - 1, 1)
                add_y(r, T - 2, 0)
                add_y(r, T - 1, 1)

        @block.tensor
        def _(pe):
            pe.wait_ge(weights_ready, 1)
            R = pe.value_load(rounds_i[0:1, 0:1], min_val=1, max_val=NPAD // P)
            pe.sem_inc(hid_done, 2)
            pe.sem_inc(w_done, 2)
            pe.sem_inc(seg_done, 2)

            def hidden(r, k, j, p):
                pe.wait_ge(e_in[p], 32 * (r * (T // 2) + k + 1))
                pe.wait_ge(silu_done, r * T + j + 1)
                nc.tensor.matmul(psE[:], w0[:], e_st[p][:], start=True, stop=True).then_inc(hid_done, 1)

            def radial(r, j, p):
                pe.wait_ge(low_done, r * T + j + 1 + 2)
                pe.wait_ge(prod_done, (r * T + j) * C + C)
                for c in range(C):
                    o = psW[p][c // 2][:, 256 * (c % 2):256 * (c % 2) + 256]
                    nc.tensor.matmul(o, hidT[p][:, P * c:P * c + P], w1hi[:], start=True, stop=False)
                    ins = nc.tensor.matmul(o, hidT[p][:, P * c:P * c + P], w1lo[:], start=False, stop=True)
                ins.then_inc(w_done, 1)

            def segment(r, j, p):
                pe.wait_ge(hots_done, r * T + j + 1 + 2)
                pe.wait_ge(y_done, r * T + j + 1)
                y = psY[p][:, :].rearrange("p (a u) -> p a u", u=MUL)
                for c in range(C):
                    pe.wait_ge(prod_done, (r * T + j) * C + c + 1 + 2 * C)
                    a = prod[p][:, c, :].rearrange("p (a u) -> p a u", u=MUL)
                    ins = nc.tensor.matmul(y[:, 1::2, :], hots[p][:, 4 * c, :], a[:, 4:8, :], start=(c == 0),
                                           stop=(c == C - 1), skip_group_check=True)
                    for k in range(3):
                        ins = nc.tensor.matmul(y[:, 2 * k::6 - 2 * k, :][:, 0:2, :], hots[p][:, 4 * c + k + 1, :],
                                               a[:, 0::k + 1, :][:, 0:2, :], start=False, stop=(c == C - 1),
                                               skip_group_check=True)
                ins.then_inc(seg_done, 1)

            with pe.Fori(0, R) as r:
                hidden(r, 0, 0, 0)
                hidden(r, 0, 1, 1)
                radial(r, 0, 0)
                with pe.Fori(0, T // 2 - 1) as k:
                    for p in range(2):
                        t = k * 2 + p
                        hidden(r, k + 1, t + 2, p)
                        radial(r, t + 1, 1 - p)
                        segment(r, t, p)
                radial(r, T - 1, 1)
                segment(r, T - 2, 0)
                segment(r, T - 1, 1)



def update_block(nc, v):
    x_sb, s_sb, y_sb, zo, ident, logits = v["x_sb"], v["s_sb"], v["y_sb"], v["zo"], v["ident"], v["logits"]
    xnew_d, xn_d, xT_d = v["xnew_d"], v["xn_d"], v["xT_d"]

    with ExitStack() as ctx:
        def sb(name, shape, dt=F32):
            return ctx.enter_context(nc.sbuf_tensor(name, shape, dt))

        def pb(name):
            return ctx.enter_context(nc.psum_tensor(name, [P, 512], F32))

        def sem(name):
            return ctx.enter_context(nc.semaphore(name))

        w2 = sb("u_w2", [P, 4, MUL])
        wr = sb("u_wr", [P, KC, EXPERTS])
        eps = sb("u_eps", [P, 1])
        ys = sb("u_ys", [P, GROUP, 512])
        yT = sb("u_yT", [P, 2, 512])
        gnn = sb("u_gnn", [P, GROUP, FEAT])
        stats = sb("u_stats", [P, GROUP, 6])
        mv = sb("u_mv", [P, GROUP, 2])
        root = sb("u_root", [P, GROUP])
        rstd = sb("u_rstd", [P, GROUP])
        xn = sb("u_xn", [P, GROUP, FEAT])
        xT = sb("u_xT", [P, 2, KC, P])
        xhi = sb("u_xhi", [P, KC, SH], F32R)
        xlo = sb("u_xlo", [P, KC, SH], F32R)
        psY = [pb(f"u_psY{i}") for i in range(2)]
        psO = [pb(f"u_psO{i}") for i in range(2)]
        psX = [pb(f"u_psX{i}") for i in range(2)]
        psL = [pb(f"u_psL{i}") for i in range(2)]

        w_in, rows_out, cols_out = sem("u_w_in"), sem("u_rows_out"), sem("u_cols_out")
        w_ready, staged, turned, yT_ready = sem("u_w_ready"), sem("u_staged"), sem("u_turned"), sem("u_yT_ready")
        mixed, gnn_done, x_done, stats_done = sem("u_mixed"), sem("u_gnn_done"), sem("u_x_done"), sem("u_stats_done")
        aggr_go, aggr_done, root_done = sem("u_aggr_go"), sem("u_aggr_done"), sem("u_root_done")
        rstd_done, xn_done, x_turned = sem("u_rstd_done"), sem("u_xn_done"), sem("u_x_turned")
        xT_ready, hi_done, lo_done, scored = sem("u_xT_ready"), sem("u_hi_done"), sem("u_lo_done"), sem("u_scored")
        logits_done, rows_free, cols_free = sem("u_logits_done"), sem("u_rows_free"), sem("u_cols_free")
        block = ctx.enter_context(nc.Block())


        @block.sync
        def _(sp):
            for c in range(3):
                sp.dma_start(w2[:, c, :], v["w_21"]).then_inc(w_in, 16)
            sp.dma_start(w2[0:MUL, 3, :], v["w_20"][MUL:2 * MUL, :]).then_inc(w_in, 16)
            sp.dma_start(w2[MUL:P, 3, :], v["w_20"][0:MUL, :]).then_inc(w_in, 16)
            sp.dma_start(wr[:], v["w_r"].rearrange("(k p) e -> p k e", p=P)).then_inc(w_in, 16)
            sp.sem_inc(rows_free, 1)
            sp.sem_inc(cols_free, 1)
            with sp.Fori(0, NG) as g:
                first = sp.snap(g * GROUP)
                first_col = sp.snap(g * SH)
                sp.wait_ge(xn_done, (g + 1) * GROUP)
                for src, dst in ((x_sb[:, at(first, GROUP), :], xnew_d), (xn[:], xn_d)):
                    sp.dma_start(dst.rearrange("(t p) f -> p t f", p=P)[:, at(first, GROUP), :], src
                                 ).then_inc(rows_out, 16)
                sp.wait_ge(rows_out, 32 * (g + 1))
                sp.sem_inc(rows_free, 1)
                sp.wait_ge(lo_done, (g + 1) * GROUP)
                for h, part in enumerate((xhi, xlo)):
                    sp.dma_start(xT_d[h, :, :, at(first_col, SH)], part[:].bitcast(F32)).then_inc(cols_out, 16)
                sp.wait_ge(cols_out, 32 * (g + 1))
                sp.sem_inc(cols_free, 1)

        @block.vector
        def _(dve):
            nc.vector.memset(eps[:], EPS)
            dve.wait_ge(w_in, 16 * 6)
            nc.vector.tensor_scalar(w2[0:MUL, 3, :], w2[0:MUL, 3, :], INV_SQRT3, None, ALU.mult).then_inc(w_ready, 1)
            dve.sem_inc(gnn_done, 1)
            with dve.Fori(0, NG) as g:
                for j in range(GROUP):
                    dve.wait_ge(turned, g * GROUP + j + 1)
                    nc.vector.tensor_copy(ys[:, j, :], y_sb[:, at(g * GROUP + j), :, :].rearrange("p o a u -> p (o a u)")
                                          ).then_inc(staged, 1)
                for j in range(GROUP):
                    t = g * GROUP + j
                    dve.wait_ge(mixed, t + 1 + 2)
                    nc.vector.scalar_tensor_tensor(
                        out=gnn[:, j, :], in0=psO[j % 2][:, 0:FEAT], scalar=zo[:, at(t)],
                        in1=s_sb[:, at(t), :].rearrange("p o f -> p (o f)"), op0=ALU.mult, op1=ALU.add
                    ).then_inc(gnn_done, 1)
                for j in range(GROUP):
                    t = g * GROUP + j
                    dve.wait_ge(gnn_done, t + 1 + 1)
                    row = x_sb[:, at(t), :].rearrange("p o f -> p (o f)")
                    nc.vector.tensor_tensor(row[:, 0:MUL], row[:, 0:MUL], gnn[:, j, 0:MUL], ALU.add)
                    cols = row[:, MUL:].rearrange("p (u c) -> p u c", c=3)
                    nc.vector.tensor_tensor(cols, cols, gnn[:, j, MUL:].rearrange("p (c u) -> p u c", c=3),
                                            ALU.add).then_inc(x_done, 1)
                for j in range(GROUP):
                    t = g * GROUP + j
                    dve.wait_ge(x_done, t + 1)
                    dve.sem_inc(aggr_go, 1)
                    ins = nc.vector.bn_stats(stats[:, j, :], x_sb[:, at(t), :].rearrange("p o f -> p (o f)"))
                ins.then_inc(stats_done, 1)
                dve.wait_ge(stats_done, g + 1)
                dve.sem_inc(aggr_go, 1)
                for j in range(GROUP):
                    ins = nc.vector.bn_aggr(mv[:, j, :], stats[:, j, :])
                ins.then_inc(aggr_done, 1)
                dve.wait_ge(root_done, g + 1)
                nc.vector.reciprocal(rstd[:], root[:]).then_inc(rstd_done, 1)
                dve.wait_ge(rstd_done, g + 1)
                dve.wait_ge(rows_free, g + 1)
                dve.wait_ge(x_turned, g * GROUP + GROUP)
                for j in range(GROUP):
                    t = g * GROUP + j
                    nc.vector.tensor_scalar(xn[:, j, :], x_sb[:, at(t), :].rearrange("p o f -> p (o f)"), mv[:, j, 0:1],
                                            rstd[:, j:j + 1], ALU.subtract, ALU.mult).then_inc(xn_done, 1)
                for j in range(GROUP):
                    t = g * GROUP + j
                    dve.wait_ge(hi_done, t + 1)
                    nc.vector.tensor_tensor(xlo[:, :, P * j:P * j + P], xT[:, j % 2, :, :],
                                            xhi[:, :, P * j:P * j + P].bitcast(F32), ALU.subtract).then_inc(lo_done, 1)

        @block.scalar
        def _(act):
            act.sem_inc(yT_ready, 1)
            act.sem_inc(xT_ready, 1)
            act.sem_inc(logits_done, 1)
            with act.Fori(0, NG) as g:
                for j in range(GROUP):
                    t = g * GROUP + j
                    act.wait_ge(turned, t + 1 + GROUP)
                    act.wait_ge(mixed, t + 2 if j == 0 else t + 1)
                    nc.scalar.activation(yT[:, j % 2, :], psY[j % 2][:], ACT.Copy).then_inc(yT_ready, 1)
                act.wait_ge(aggr_done, g + 1)
                nc.scalar.activation(root[:], mv[:, :, 1], ACT.Sqrt, bias=eps[:]).then_inc(root_done, 1)
                act.wait_ge(cols_free, g + 1)
                for j in range(GROUP):
                    t = g * GROUP + j
                    act.wait_ge(x_turned, t + 1 + GROUP)
                    act.wait_ge(scored, t + 2 if j == 0 else t + 1)
                    if j > 1:
                        act.wait_ge(lo_done, t - 1)
                    nc.scalar.activation(xT[:, j % 2, :, :].rearrange("p k n -> p (k n)"), psX[j % 2][:, 0:FEAT],
                                         ACT.Copy).then_inc(xT_ready, 1)
                    act.wait_ge(xT_ready, t + 1 + 1)
                    nc.scalar.activation(xhi[:, :, P * j:P * j + P], xT[:, j % 2, :, :], ACT.Copy).then_inc(hi_done, 1)
                    act.wait_ge(scored, t + 1 + 2)
                    nc.scalar.activation(logits[:, at(t), :].rearrange("p o e -> p (o e)"), psL[j % 2][:, 0:EXPERTS],
                                         ACT.Copy).then_inc(logits_done, 1)

        @block.tensor
        def _(pe):
            pe.wait_ge(w_ready, 1)
            pe.sem_inc(turned, GROUP)
            pe.sem_inc(x_turned, GROUP)
            pe.sem_inc(mixed, 2)
            pe.sem_inc(scored, 2)
            with pe.Fori(0, NG) as g:
                def turn(j):
                    t = g * GROUP + j
                    pe.wait_ge(staged, t + 1)
                    pe.wait_ge(yT_ready, t + 1 if j == 0 else t)
                    for c in range(4):
                        ins = nc.tensor.transpose(psY[j % 2][:, P * c:P * c + P], ys[:, j, P * c:P * c + P], ident[:])
                    ins.then_inc(turned, 1)

                def mix(j):
                    t = g * GROUP + j
                    pe.wait_ge(yT_ready, t + 2)
                    pe.wait_ge(gnn_done, t + 1 if j == 0 else t)
                    for c in range(4):
                        o = MUL * (c + 1) if c < 3 else 0
                        ins = nc.tensor.matmul(psO[j % 2][:, o:o + MUL], yT[:, j % 2, P * c:P * c + P], w2[:, c, :],
                                               start=True, stop=True)
                    ins.then_inc(mixed, 1)

                def turn_x(j):
                    t = g * GROUP + j
                    pe.wait_ge(xn_done, t + 1)
                    pe.wait_ge(xT_ready, t + 1 if j == 0 else t)
                    for k in range(KC):
                        ins = nc.tensor.transpose(psX[j % 2][:, P * k:P * k + P], xn[:, j, P * k:P * k + P], ident[:])
                    ins.then_inc(x_turned, 1)

                def score(j):
                    t = g * GROUP + j
                    pe.wait_ge(xT_ready, t + 2)
                    pe.wait_ge(logits_done, t + 1 if j == 0 else t)
                    for k in range(KC):
                        ins = nc.tensor.matmul(psL[j % 2][:, 0:EXPERTS], xT[:, j % 2, k, :], wr[:, k, :],
                                               start=(k == 0), stop=(k == KC - 1))
                    ins.then_inc(scored, 1)

                turn(0)
                for j in range(GROUP):
                    if j + 1 < GROUP:
                        turn(j + 1)
                    mix(j)
                turn_x(0)
                for j in range(GROUP):
                    if j + 1 < GROUP:
                        turn_x(j + 1)
                    score(j)


def route_block(nc, v):
    logits, ones, earlier = v["logits"], v["ones"], v["earlier"]
    counts_i, pos_i, meta_i = v["counts_i"], v["pos_i"], v["meta_i"]
    E = EXPERTS
    TALL = [P, NT, E]

    with ExitStack() as ctx:
        def sb(name, shape, dt=F32):
            return ctx.enter_context(nc.sbuf_tensor(name, shape, dt))

        def sem(name):
            return ctx.enter_context(nc.semaphore(name))

        falling = sb("r_falling", [P, E])
        token_i = sb("r_token", [P, NT], I32)
        top = sb("r_top", [P, NT])
        shifted = sb("r_shifted", TALL)
        expd = sb("r_expd", TALL)
        total = sb("r_total", [P, NT])
        inverse = sb("r_inverse", [P, NT])
        gate = sb("r_gate", TALL)
        rest = sb("r_rest", TALL)
        best = [sb(f"r_best{k}", [P, NT]) for k in range(2)]
        same = sb("r_same", TALL)
        pick = sb("r_pick", [P, NT])
        hot = [sb(f"r_hot{k}", TALL) for k in range(2)]
        chosen = sb("r_chosen", TALL)
        rank = sb("r_rank", TALL)
        per_tile = sb("r_per_tile", TALL)
        running = [sb(f"r_running{k}", TALL) for k in range(2)]
        slot = sb("r_slot", TALL)
        mine = sb("r_mine", TALL)
        need_i = sb("r_need_i", [P, E], I32)
        need = sb("r_need", [P, E])
        need_f = sb("r_need_f", [P, E])
        ends = [sb(f"r_ends{k}", [P, E]) for k in range(2)]
        start = sb("r_start", [P, E])
        pos = sb("r_pos", [P, NT])
        weight = sb("r_weight", [P, NT])
        psR = ctx.enter_context(nc.psum_tensor("r_psR", [P, 512], F32))
        psT = ctx.enter_context(nc.psum_tensor("r_psT", [P, 512], F32))

        consts, step, shift_done, exp_done = sem("r_consts"), sem("r_step"), sem("r_shift_done"), sem("r_exp_done")
        chosen_done, counted = sem("r_chosen_done"), sem("r_counted")
        block = ctx.enter_context(nc.Block())

        def wide(a):
            return a.unsqueeze(2).to_broadcast(TALL)

        @block.gpsimd
        def _(pool):
            pool.iota(falling[:], [[-1, E]], base=E, channel_multiplier=0, allow_small_or_imprecise_dtypes=True)
            pool.iota(token_i[:], [[P, NT]], base=0, channel_multiplier=1).then_inc(consts, 1)

        @block.scalar
        def _(act):
            act.wait_ge(shift_done, 1)
            nc.scalar.activation(expd[:], shifted[:], ACT.Exp).then_inc(exp_done, 1)

        @block.tensor
        def _(pe):
            pe.wait_ge(chosen_done, 1)
            flat = chosen[:].rearrange("p t e -> p (t e)")
            nc.tensor.matmul(psR[:, 0:NT * E], earlier[:], flat, start=True, stop=True)
            nc.tensor.matmul(psT[:, 0:NT * E], ones[:], flat, start=True, stop=True).then_inc(counted, 1)

        @block.vector
        def _(dve):
            link = chain_of(dve, step)
            link(nc.vector.tensor_reduce(top[:], logits[:], AX_X, ALU.max))
            link(nc.vector.tensor_tensor(shifted[:], logits[:], wide(top[:]), ALU.subtract))
            dve.sem_inc(shift_done, 1)
            dve.wait_ge(exp_done, 1)
            link(nc.vector.tensor_reduce(total[:], expd[:], AX_X, ALU.add))
            link(nc.vector.reciprocal(inverse[:], total[:]))
            link(nc.vector.tensor_tensor(gate[:], expd[:], wide(inverse[:]), ALU.mult))
            dve.wait_ge(consts, 1)
            for k, values in enumerate((gate, rest)):
                link(nc.vector.tensor_reduce(best[k][:], values[:], AX_X, ALU.max))
                link(nc.vector.tensor_tensor(same[:], values[:], wide(best[k][:]), ALU.is_equal))
                link(nc.vector.tensor_tensor(same[:], same[:], falling[:].unsqueeze(1).to_broadcast(TALL), ALU.mult))
                link(nc.vector.tensor_reduce(pick[:], same[:], AX_X, ALU.max))
                link(nc.vector.tensor_tensor(hot[k][:], falling[:].unsqueeze(1).to_broadcast(TALL), wide(pick[:]),
                                             ALU.is_equal))
                if k == 0:
                    link(nc.vector.scalar_tensor_tensor(out=rest[:], in0=hot[0][:], scalar=-4.0, in1=gate[:],
                                                        op0=ALU.mult, op1=ALU.add))
            link(nc.vector.tensor_tensor(chosen[:], hot[0][:], hot[1][:], ALU.add))
            dve.sem_inc(chosen_done, 1)
            link(nc.vector.tensor_tensor(total[:], best[0][:], best[1][:], ALU.add))
            link(nc.vector.reciprocal(inverse[:], total[:]))
            for k in range(2):
                link(nc.vector.tensor_tensor(weight[:], best[k][:], inverse[:], ALU.mult))
                link(nc.vector.tensor_copy(meta_i[:, :, k, 1].bitcast(F32), weight[:]))
                link(nc.vector.tensor_copy(meta_i[:, :, k, 0], token_i[:]))
            dve.wait_ge(counted, 1)
            link(nc.vector.tensor_copy(rank[:].rearrange("p t e -> p (t e)"), psR[:, 0:NT * E]))
            link(nc.vector.tensor_copy(per_tile[:].rearrange("p t e -> p (t e)"), psT[:, 0:NT * E]))
            link(nc.vector.tensor_copy(running[0][:], per_tile[:]))
            now, d = 0, 1
            while d < NT:
                a, b = running[now], running[1 - now]
                link(nc.vector.tensor_copy(b[:, 0:d, :], a[:, 0:d, :]))
                link(nc.vector.tensor_tensor(b[:, d:, :], a[:, d:, :], a[:, 0:NT - d, :], ALU.add))
                now, d = 1 - now, 2 * d
            run = running[now]
            link(nc.vector.tensor_scalar(need[:], run[:, NT - 1, :], float(TOK - 1), None, ALU.add))
            link(nc.vector.tensor_copy(need_i[:], need[:]))
            link(nc.vector.tensor_single_scalar(need_i[:], need_i[:], TOK.bit_length() - 1, ALU.logical_shift_right))
            link(nc.vector.tensor_copy(need_f[:], need_i[:]))
            link(nc.vector.tensor_scalar(need[:], need_f[:], 1.0, None, ALU.max))
            link(nc.vector.tensor_copy(ends[0][:], need[:]))
            at_, d = 0, 1
            while d < E:
                a, b = ends[at_], ends[1 - at_]
                link(nc.vector.tensor_copy(b[:, 0:d], a[:, 0:d]))
                link(nc.vector.tensor_tensor(b[:, d:], a[:, d:], a[:, 0:E - d], ALU.add))
                at_, d = 1 - at_, 2 * d
            link(nc.vector.tensor_tensor(start[:], ends[at_][:], need[:], ALU.subtract))
            link(nc.vector.tensor_copy(counts_i[:, 0:E], need[0:1, :]))
            link(nc.vector.tensor_copy(counts_i[:, E:2 * E], start[0:1, :]))
            link(nc.vector.tensor_tensor(slot[:], run[:], per_tile[:], ALU.subtract))
            link(nc.vector.tensor_tensor(slot[:], slot[:], rank[:], ALU.add))
            link(nc.vector.scalar_tensor_tensor(out=slot[:], in0=start[:].unsqueeze(1).to_broadcast(TALL),
                                                scalar=float(TOK), in1=slot[:], op0=ALU.mult, op1=ALU.add))
            for k in range(2):
                link(nc.vector.tensor_tensor(mine[:], slot[:], hot[k][:], ALU.mult))
                link(nc.vector.tensor_reduce(pos[:], mine[:], AX_X, ALU.add))
                link(nc.vector.tensor_copy(pos_i[:, :, k], pos[:]))


def load_weights(eng, raw, w1, w2, e, sem):
    eng.dma_start(raw[:, 0:KC * HID].rearrange("p (k f) -> p k f", k=KC),
                  w1[at(e)].rearrange("o (k p) f -> p (o k) f", p=P)).then_inc(sem, 16)
    eng.dma_start(raw[:, KC * HID:].rearrange("p (k f) -> p k f", k=FC),
                  w2[at(e)].rearrange("o (k p) f -> p (o k) f", p=P)).then_inc(sem, 16)


def expert_blocks(nc, v):
    with ExitStack() as ctx:
        def sb(name, shape, dt=F32):
            return ctx.enter_context(nc.sbuf_tensor(name, shape, dt))

        WW = KC * HID + FC * FEAT
        raw = sb("x_raw", [P, WW])
        whi = [sb(f"x_whi{i}", [P, WW], F32R) for i in range(2)]
        wlo = [sb(f"x_wlo{i}", [P, WW], F32R) for i in range(2)]
        b1_sb = sb("x_b1", [P, EXPERTS + 1, FC])
        b2_sb = sb("x_b2", [P, EXPERTS + 1, FEAT])
        w_in, whi_done, wlo_done = (ctx.enter_context(nc.semaphore(n)) for n in ("w_in", "whi_done", "wlo_done"))
        shared = dict(v, w_in=w_in, whi_done=whi_done, wlo_done=wlo_done, raw=raw, whi=whi, wlo=wlo, b1_sb=b1_sb, b2_sb=b2_sb)
        shared_block(nc, shared)
        routed_block(nc, shared)


def w1_part(w, k, f):
    return w[:, k * HID + P * f:k * HID + P * f + P]


def w2_part(w, f):
    return w[:, KC * HID + FEAT * f:KC * HID + FEAT * f + FEAT]


def up_product(nc, ps, whi, wlo, xhi, xlo, f):
    terms = [(w, x, k) for k in range(KC) for w, x in ((whi, xhi), (whi, xlo), (wlo, xhi))]
    for n, (w, x, k) in enumerate(terms):
        ins = nc.tensor.matmul(ps, w1_part(w, k, f), x(k), start=(n == 0), stop=(n == len(terms) - 1))
    return ins


def down_product(nc, ps, hhi, hlo, whi, wlo, f):
    for n, (h, w) in enumerate(((hhi, whi), (hhi, wlo), (hlo, whi))):
        ins = nc.tensor.matmul(ps, h, w2_part(w, f), start=(f == 0 and n == 0), stop=(f == FC - 1 and n == 2))
    return ins


def shared_block(nc, v):
    raw, whi, wlo, b1_sb, b2_sb = v["raw"], v["whi"], v["wlo"], v["b1_sb"], v["b2_sb"]
    w1, w2, out, xT_d, xnew_d, xn_d, slots_d = (v[k] for k in ("w1", "w2", "out", "xT_d", "xnew_d", "xn_d", "slots_d"))
    pos_i, meta_i = v["pos_i"], v["meta_i"]

    with ExitStack() as ctx:
        def sb(name, shape, dt=F32):
            return ctx.enter_context(nc.sbuf_tensor(name, shape, dt))

        def pb(name):
            return ctx.enter_context(nc.psum_tensor(name, [P, 512], F32))

        def sem(name):
            return ctx.enter_context(nc.semaphore(name))

        xhi = sb("s_xhi", [P, KC, SH], F32R)
        xlo = sb("s_xlo", [P, KC, SH], F32R)
        xnew = sb("s_xnew", [P, GROUP, FEAT])
        hf = [sb(f"s_hf{i}", [P, SHH]) for i in range(4)]
        hhi = sb("s_hhi", [P, FC, SH], F32R)
        hlo = sb("s_hlo", [P, FC, SH], F32R)
        biased = sb("s_biased", [P, 2, FEAT])
        ob = sb("s_ob", [P, GROUP, FEAT])
        row = [[sb(f"s_row{j}{k}", [P, ROW]) for k in range(2)] for j in range(GROUP)]
        pos_st = [sb(f"s_pos{j}", [P, 2], I32) for j in range(GROUP)]
        psA = [pb(f"s_psA{i}") for i in range(4)]
        psB = [pb(f"s_psB{i}") for i in range(2)]

        w_in, whi_done, wlo_done = v["w_in"], v["whi_done"], v["wlo_done"]
        b_in, xT_in, xnew_in, o_out = sem("s_b_in"), sem("s_xT_in"), sem("s_xnew_in"), sem("s_o_out")
        row_in = [sem(f"s_row_in{j}") for j in range(GROUP)]
        sent = [sem(f"s_sent{j}") for j in range(GROUP)]
        row_free, ob_free, row_go, pos_staged = sem("s_row_free"), sem("s_ob_free"), sem("s_row_go"), sem("s_pos_staged")
        up_done, gelu_done, hhi_done, hlo_done = sem("s_up_done"), sem("s_gelu_done"), sem("s_hhi_done"), sem("s_hlo_done")
        down_done, biased_done, ob_done = sem("s_down_done"), sem("s_biased_done"), sem("s_ob_done")
        block = ctx.enter_context(nc.Block())
        UP = 2 * FC


        @block.sync
        def _(sp):
            load_weights(sp, raw, w1, w2, 0, w_in)
            sp.dma_start(b1_sb[:].rearrange("p e f -> p (e f)"), v["b1"]).then_inc(b_in, 16)
            sp.dma_start(b2_sb[:], v["b2"].rearrange("(o e) f -> o e f", o=1).to_broadcast([P, EXPERTS + 1, FEAT])
                         ).then_inc(b_in, 16)

            def load_group(g):
                for h, part in enumerate((xhi, xlo)):
                    sp.dma_start(part[:].bitcast(F32), xT_d[h, :, :, at(g * SH, SH)]).then_inc(xT_in, 16)

            def load_rows(g, j):
                for k in range(2):
                    sp.dma_start(row[j][k][:, 0:FEAT], xn_d[at((g * GROUP + j) * P, P), :]).then_inc(row_in[j], 16)

            def load_xnew(g):
                sp.dma_start(xnew[:], xnew_d.rearrange("(t p) f -> p t f", p=P)[:, at(g * GROUP, GROUP), :]
                             ).then_inc(xnew_in, 16)

            def store(g):
                sp.dma_start(out[0:NPAD, :].rearrange("(t p) f -> p t f", p=P)[:, at(g * GROUP, GROUP), :], ob[:]
                             ).then_inc(o_out, 16)

            load_group(0)
            load_xnew(0)
            for j in range(GROUP):
                load_rows(0, j)
            sp.wait_ge(wlo_done, 1)
            load_weights(sp, raw, w1, w2, 1, w_in)
            sp.sem_inc(ob_free, 1)
            with sp.Fori(0, NG - 1) as h:
                g = sp.snap(h + 1)
                col = sp.snap(g * SH)
                sp.wait_ge(up_done, g * UP)
                for i, part in enumerate((xhi, xlo)):
                    sp.dma_start(part[:].bitcast(F32), xT_d[i, :, :, at(col, SH)]).then_inc(xT_in, 16)
                for j in range(GROUP):
                    first = sp.snap((g * GROUP + j) * P)
                    sp.wait_ge(row_free, g * GROUP + j + 1)
                    for k in range(2):
                        sp.dma_start(row[j][k][:, 0:FEAT], xn_d[at(first, P), :]).then_inc(row_in[j], 16)
                tile = sp.snap(g * GROUP)
                before = sp.snap(h * GROUP)
                sp.wait_ge(ob_done, g * GROUP + 1)
                sp.dma_start(out[0:NPAD, :].rearrange("(t p) f -> p t f", p=P)[:, at(before, GROUP), :], ob[:]
                             ).then_inc(o_out, 16)
                sp.dma_start(xnew[:], xnew_d.rearrange("(t p) f -> p t f", p=P)[:, at(tile, GROUP), :]
                             ).then_inc(xnew_in, 16)
                sp.wait_ge(o_out, 16 * g)
                sp.sem_inc(ob_free, 1)
            sp.wait_ge(wlo_done, 2)
            load_weights(sp, raw, w1, w2, 2, w_in)
            sp.wait_ge(ob_done, NT + 1)
            store(NG - 1)
            sp.wait_ge(o_out, 16 * NG)
            sp.wait_ge(w_in, 32 * 3)

        @block.gpsimd
        def _(pool):
            pool.sem_inc(row_free, GROUP)
            with pool.Fori(0, NG) as g:
                for j in range(GROUP):
                    t = g * GROUP + j
                    pool.wait_ge(row_free, g * GROUP + GROUP)
                    pool.tensor_copy(pos_st[j][:], pos_i[:, at(t), :].rearrange("p o k -> p (o k)"))
                    for k in range(2):
                        ins = pool.tensor_copy(row[j][k][:, FEAT:ROW].bitcast(I32),
                                               meta_i[:, at(t), k, :].rearrange("p o m -> p (o m)"))
                    ins.then_inc(pos_staged, 1)
                for j in range(GROUP):
                    t = g * GROUP + j
                    pool.wait_ge(pos_staged, t + 1)
                    pool.wait_ge(row_in[j], 32 * (g + 1))
                    pool.sem_inc(row_go, 1)
                    for k in range(2):
                        pool.indirect_dma_start(
                            out=slots_d, out_offset=bass.IndirectOffsetOnAxis(ap=pos_st[j][:, k:k + 1], axis=0),
                            in_=row[j][k][:], in_offset=None).then_inc(sent[j], 16)
                for j in range(GROUP):
                    pool.wait_ge(sent[j], 32 * (g + 1))
                    pool.sem_inc(row_free, 1)

        @block.scalar
        def _(act):
            act.sem_inc(gelu_done, 4)
            act.wait_ge(w_in, 32)
            nc.scalar.activation(whi[0][:], raw[:], ACT.Copy).then_inc(whi_done, 1)
            act.wait_ge(b_in, 32)
            with act.Fori(0, NG) as g:
                for i in range(UP):
                    f, half = i // 2, i % 2
                    act.wait_ge(up_done, g * UP + i + 1)
                    act.wait_ge(hlo_done, g * UP + i + 1)
                    nc.scalar.activation(hf[i % 4][:], psA[i % 4][:, 0:SHH], ACT.Gelu, bias=b1_sb[:, 0, f:f + 1]
                                         ).then_inc(gelu_done, 1)
            act.wait_ge(w_in, 64)
            nc.scalar.activation(whi[1][:], raw[:], ACT.Copy).then_inc(whi_done, 1)

        @block.vector
        def _(dve):
            dve.sem_inc(hlo_done, 4)
            dve.sem_inc(ob_done, 1)
            dve.wait_ge(whi_done, 1)
            nc.vector.tensor_tensor(wlo[0][:], raw[:], whi[0][:].bitcast(F32), ALU.subtract).then_inc(wlo_done, 1)
            with dve.Fori(0, NG) as g:
                dve.wait_ge(down_done, g * GROUP + GROUP)
                for i in range(UP):
                    f, half = i // 2, i % 2
                    cols = slice(SHH * half, SHH * half + SHH)
                    dve.wait_ge(gelu_done, g * UP + i + 1 + 4)
                    nc.vector.tensor_copy(hhi[:, f, cols], hf[i % 4][:]).then_inc(hhi_done, 1)
                    dve.wait_ge(hhi_done, g * UP + i + 1)
                    nc.vector.tensor_tensor(hlo[:, f, cols], hf[i % 4][:], hhi[:, f, cols].bitcast(F32),
                                            ALU.subtract).then_inc(hlo_done, 1)
                dve.wait_ge(xnew_in, 16 * (g + 1))
                dve.wait_ge(ob_free, g + 1)
                for j in range(GROUP):
                    t = g * GROUP + j
                    dve.wait_ge(down_done, t + 1 + GROUP)
                    nc.vector.tensor_tensor(biased[:, j % 2, :], psB[j % 2][:, 0:FEAT], b2_sb[:, 0, :], ALU.add
                                            ).then_inc(biased_done, 1)
                    dve.wait_ge(biased_done, t + 1)
                    nc.vector.tensor_tensor(ob[:, j, :], biased[:, j % 2, :], xnew[:, j, :], ALU.add
                                            ).then_inc(ob_done, 1)
            dve.wait_ge(whi_done, 2)
            nc.vector.tensor_tensor(wlo[1][:], raw[:], whi[1][:].bitcast(F32), ALU.subtract).then_inc(wlo_done, 1)

        @block.tensor
        def _(pe):
            pe.wait_ge(wlo_done, 1)
            pe.sem_inc(down_done, GROUP)
            with pe.Fori(0, NG) as g:
                pe.wait_ge(xT_in, 32 * (g + 1))
                for i in range(UP):
                    f, half = i // 2, i % 2
                    pe.wait_ge(gelu_done, g * UP + i + 1)
                    up_product(nc, psA[i % 4][:, 0:SHH], whi[0], wlo[0],
                               lambda k, half=half: xhi[:, k, SHH * half:SHH * half + SHH],
                               lambda k, half=half: xlo[:, k, SHH * half:SHH * half + SHH], f).then_inc(up_done, 1)
                for j in range(GROUP):
                    t = g * GROUP + j
                    pe.wait_ge(hlo_done, (g + 1) * UP + 4)
                    pe.wait_ge(ob_done, t + 1 if j == 0 else t)
                    for f in range(FC):
                        ins = down_product(nc, psB[j % 2][:, 0:FEAT], hhi[:, f, P * j:P * j + P],
                                           hlo[:, f, P * j:P * j + P], whi[0], wlo[0], f)
                    ins.then_inc(down_done, 1)


def routed_block(nc, v):
    raw, whi, wlo, b1_sb, b2_sb = v["raw"], v["whi"], v["wlo"], v["b1_sb"], v["b2_sb"]
    w1, w2, out, slots_d, ident, counts_i = (v[k] for k in ("w1", "w2", "out", "slots_d", "ident", "counts_i"))

    with ExitStack() as ctx:
        def sb(name, shape, dt=F32):
            return ctx.enter_context(nc.sbuf_tensor(name, shape, dt))

        def pb(name):
            return ctx.enter_context(nc.psum_tensor(name, [P, 512], F32))

        def sem(name):
            return ctx.enter_context(nc.semaphore(name))

        rows = sb("q_rows", [P, SUB, ROW])
        meta = sb("q_meta", [P, SUB, 2], I32)
        index = [sb(f"q_index{m}", [P, 1], I32) for m in range(SUB)]
        xf = sb("q_xf", [P, KC, TOK])
        xhi = sb("q_xhi", [P, KC, TOK], F32R)
        xlo = sb("q_xlo", [P, KC, TOK], F32R)
        hf = [sb(f"q_hf{i}", [P, TOK]) for i in range(4)]
        hhi = sb("q_hhi", [P, FC, TOK], F32R)
        hlo = sb("q_hlo", [P, FC, TOK], F32R)
        b1_st = sb("q_b1", [P, FC])
        b2_st = sb("q_b2", [P, FEAT])
        biased = sb("q_biased", [P, SUB, FEAT])
        ob = [sb(f"q_ob{m}", [P, FEAT]) for m in range(SUB)]
        psA = [pb(f"q_psA{i}") for i in range(4)]
        psB = [pb(f"q_psB{i}") for i in range(SUB)]
        psX = pb("q_psX")

        w_in, whi_done, wlo_done = v["w_in"], v["whi_done"], v["wlo_done"]
        rows_in, added, w_go = sem("q_rows_in"), sem("q_added"), sem("q_w_go")
        add_go, ob_free, b1_done, b2_done = sem("q_add_go"), sem("q_ob_free"), sem("q_b1_done"), sem("q_b2_done")
        turned, xf_done = sem("q_turned"), sem("q_xf_done")
        begun = sem("q_begun")
        xhi_done, xlo_done, meta_done = sem("q_xhi_done"), sem("q_xlo_done"), sem("q_meta_done")
        up_done, gelu_done, hhi_done, hlo_done = sem("q_up_done"), sem("q_gelu_done"), sem("q_hhi_done"), sem("q_hlo_done")
        down_done, biased_done, ob_done = sem("q_down_done"), sem("q_biased_done"), sem("q_ob_done")
        block = ctx.enter_context(nc.Block())


        def experts(eng, begin, tile):
            def one(e, h):
                n = eng.value_load(counts_i[0:1, at(e)], min_val=1, max_val=TILES)
                first = eng.value_load(counts_i[0:1, at(e + EXPERTS)], min_val=0, max_val=TILES)
                if begin is not None:
                    begin(e, h, first)
                if tile is not None:
                    with eng.Fori(0, n) as i:
                        s = nc.s_assert_within(first + i, 0, TILES - 1, skip_runtime_bounds_check_because=
                                               "the experts' tiles add up to TILES at most")
                        tile(s, h)

            with eng.Fori(0, EXPERTS // 2 - 1) as pair:
                one(pair * 2, 0)
                one(pair * 2 + 1, 1)
            one(EXPERTS - 2, 0)
            one(EXPERTS - 1, 1)

        slot_rows = slots_d.rearrange("(n m p) f -> n p m f", m=SUB, p=P)

        @block.sync
        def _(sp):
            sp.dma_start(rows[:], slot_rows[0]).then_inc(rows_in, 16)

            def begin(e, h, first):
                if isinstance(e, int):
                    return
                sp.wait_ge(wlo_done, e + 3)
                sp.sem_inc(w_go, 1)
                load_weights(sp, raw, w1, w2, e + 3, w_in)

            def tile(s, h):
                first_row = sp.snap((s + 1) * TOK)
                sp.wait_ge(meta_done, s + 1)
                sp.dma_start(rows[:], slots_d[at(first_row, TOK), :].rearrange("(m p) f -> p m f", p=P)
                             ).then_inc(rows_in, 16)

            experts(sp, begin, tile)

        @block.gpsimd
        def _(pool):
            pool.sem_inc(ob_free, SUB)

            def tile(s, h):
                for m in range(SUB):
                    pool.wait_ge(ob_done, s * SUB + m + 1 + SUB)
                    pool.sem_inc(add_go, 1)
                    pool.indirect_dma_start(
                        out=out, out_offset=bass.IndirectOffsetOnAxis(ap=index[m][:], axis=0),
                        in_=ob[m][:], in_offset=None, compute_op=ALU.add).then_inc(added, 16)
                    pool.wait_ge(added, (s * SUB + m + 1) * 16)
                    pool.sem_inc(ob_free, 1)

            experts(pool, None, tile)

        @block.scalar
        def _(act):
            act.sem_inc(gelu_done, 4)
            act.wait_ge(turned, 1)
            nc.scalar.activation(xf[:].rearrange("p k n -> p (k n)"), psX[:], ACT.Copy).then_inc(xf_done, 1)

            def begin(e, h, first):
                act.wait_ge(gelu_done, first * FC + 4)
                nc.scalar.activation(b1_st[:], b1_sb[:, at(e + 1), :].rearrange("p o f -> p (o f)"), ACT.Copy
                                     ).then_inc(b1_done, 1)
                if not (isinstance(e, int) and e == EXPERTS - 1):
                    act.wait_ge(down_done, first * SUB + SUB)
                    act.wait_ge(w_in, e * 32 + 32 * 3)
                    nc.scalar.activation(whi[h][:], raw[:], ACT.Copy).then_inc(whi_done, 1)
                act.wait_ge(b1_done, e + 1)
                act.sem_inc(begun, 1)

            def tile(s, h):
                for f in range(FC):
                    act.wait_ge(up_done, s * FC + f + 1)
                    act.wait_ge(hlo_done, s * FC + f + 1)
                    nc.scalar.activation(hf[f % 4][:], psA[f % 4][:, 0:TOK], ACT.Gelu, bias=b1_st[:, f:f + 1]
                                         ).then_inc(gelu_done, 1)
                act.wait_ge(turned, s + 2)
                act.wait_ge(xlo_done, s + 1)
                nc.scalar.activation(xf[:].rearrange("p k n -> p (k n)"), psX[:], ACT.Copy).then_inc(xf_done, 1)

            experts(act, begin, tile)

        @block.vector
        def _(dve):
            dve.sem_inc(hlo_done, 4)
            dve.sem_inc(ob_done, SUB)

            def split_x(s):
                dve.wait_ge(xf_done, s + 1)
                nc.vector.tensor_copy(xhi[:], xf[:]).then_inc(xhi_done, 1)
                dve.wait_ge(xhi_done, s + 1)
                nc.vector.tensor_tensor(xlo[:], xf[:], xhi[:].bitcast(F32), ALU.subtract).then_inc(xlo_done, 1)

            split_x(0)
            nc.vector.tensor_copy(meta[:], rows[:, :, FEAT:ROW].bitcast(I32)).then_inc(meta_done, 1)

            def begin(e, h, first):
                dve.wait_ge(ob_done, first * SUB + SUB)
                nc.vector.tensor_copy(b2_st[:], b2_sb[:, at(e + 1), :].rearrange("p o f -> p (o f)")
                                      ).then_inc(b2_done, 1)
                if not (isinstance(e, int) and e == EXPERTS - 1):
                    dve.wait_ge(whi_done, e + 3)
                    nc.vector.tensor_tensor(wlo[h][:], raw[:], whi[h][:].bitcast(F32), ALU.subtract
                                            ).then_inc(wlo_done, 1)
                dve.wait_ge(b2_done, e + 1)
                dve.sem_inc(begun, 1)

            def tile(s, h):
                dve.wait_ge(down_done, s * SUB + SUB)
                for f in range(FC):
                    dve.wait_ge(gelu_done, s * FC + f + 1 + 4)
                    nc.vector.tensor_copy(hhi[:, f, :], hf[f % 4][:]).then_inc(hhi_done, 1)
                    dve.wait_ge(hhi_done, s * FC + f + 1)
                    nc.vector.tensor_tensor(hlo[:, f, :], hf[f % 4][:], hhi[:, f, :].bitcast(F32), ALU.subtract
                                            ).then_inc(hlo_done, 1)
                split_x(s + 1)
                dve.wait_ge(ob_free, s * SUB + SUB)
                for m in range(SUB):
                    dve.wait_ge(down_done, s * SUB + m + 1 + SUB)
                    nc.vector.tensor_copy(index[m][:], meta[:, m, 0:1])
                    nc.vector.tensor_tensor(biased[:, m, :], psB[m][:, 0:FEAT], b2_st[:], ALU.add
                                            ).then_inc(biased_done, 1)
                    dve.wait_ge(biased_done, s * SUB + m + 1)
                    nc.vector.tensor_scalar(ob[m][:], biased[:, m, :], meta[:, m, 1:2].bitcast(F32), None, ALU.mult
                                            ).then_inc(ob_done, 1)
                dve.wait_ge(ob_done, s * SUB + SUB + SUB)
                nc.vector.tensor_copy(meta[:], rows[:, :, FEAT:ROW].bitcast(I32)).then_inc(meta_done, 1)

            experts(dve, begin, tile)

        @block.tensor
        def _(pe):
            pe.sem_inc(down_done, SUB)

            def turn(s):
                pe.wait_ge(rows_in, (s + 1) * 16)
                for k in range(KC):
                    for m in range(SUB):
                        ins = nc.tensor.transpose(psX[:, TOK * k + P * m:TOK * k + P * m + P],
                                                  rows[:, m, P * k:P * k + P], ident[:])
                ins.then_inc(turned, 1)

            turn(0)

            def begin(e, h, first):
                pe.wait_ge(wlo_done, e + 2)
                pe.sem_inc(begun, 1)

            def tile(s, h):
                hi, lo = whi[1 - h], wlo[1 - h]
                pe.wait_ge(xlo_done, s + 1)
                for f in range(FC):
                    pe.wait_ge(gelu_done, s * FC + f + 1)
                    up_product(nc, psA[f % 4][:, 0:TOK], hi, lo, lambda k: xhi[:, k, :], lambda k: xlo[:, k, :], f
                               ).then_inc(up_done, 1)
                for f in range(FC):
                    pe.wait_ge(hlo_done, s * FC + f + 1 + 4)
                    if f == 0:
                        pe.wait_ge(ob_done, s * SUB + SUB)
                    if f == FC // 2:
                        pe.wait_ge(xf_done, s + 1)
                        turn(s + 1)
                    for m in range(SUB):
                        ins = down_product(nc, psB[m][:, 0:FEAT], hhi[:, f, P * m:P * m + P],
                                           hlo[:, f, P * m:P * m + P], hi, lo, f)
                        if f == FC - 1:
                            ins.then_inc(down_done, 1)

            experts(pe, begin, tile)


def kernel(**inputs):
    import concourse.bacc as bacc
    from concourse.bass_utils import run_bass_kernel_spmd

    a = {k: np.asarray(v) for k, v in inputs.items()}

    def rows(m, n, mode="constant"):
        return np.pad(m, [(0, n - m.shape[0])] + [(0, 0)] * (m.ndim - 1), mode=mode)

    src = rows(a["src"], EPAD, "edge").reshape(T * C, P).T
    dst = rows(a["dst"], EPAD, "edge")
    sh = rows(a["edge_attr_4"], EPAD).reshape(T, C, P, 4).transpose(2, 0, 1, 3).reshape(P, T * C * 4)
    fc1 = a["L0_gnn_fc_w1"]
    columns = [fc1[:, MUL * k:MUL * (k + 1)] for k in (1, 0, 3, 2)]
    b1 = np.concatenate([a["L0_ffn_b1s"][None], a["L0_ffn_b1p"]]).reshape(EXPERTS + 1, FC, P).transpose(2, 0, 1)
    arrays = {
        "x": rows(a["x"], NPAD),
        "src_t": src,
        "dst_t": dst.reshape(T * C, P).T,
        "dst_w": dst.reshape(T, STEP),
        "sh_t": sh,
        "ele_t": rows(a["edge_attr_8"], EPAD).T,
        "z_t": rows(a["node_vec1"], NPAD).reshape(NT, P).T,
        "w_sc0": a["L0_gnn_W_sc0"],
        "w_sc1": a["L0_gnn_W_sc1"],
        "w_l0": a["L0_gnn_W_lin1_0"],
        "w_l1": a["L0_gnn_W_lin1_1"],
        "fc0": np.tile(a["L0_gnn_fc_w0"], (2, 2)),
        "fc1": np.tile(np.concatenate(columns, axis=1), (2, 1)),
        "w_20": a["L0_gnn_W_lin2_0"],
        "w_21": a["L0_gnn_W_lin2_1"],
        "w_r": a["L0_ffn_Wr"],
        "w1": np.concatenate([a["L0_ffn_W1s"][None], a["L0_ffn_W1p"]]),
        "b1": b1.reshape(P, (EXPERTS + 1) * FC),
        "w2": np.concatenate([a["L0_ffn_W2s"][None], a["L0_ffn_W2p"]]),
        "b2": np.concatenate([a["L0_ffn_b2s"][None], a["L0_ffn_b2p"]]),
    }
    nc = bacc.Bacc("TRN2", target_bir_lowering=False, num_devices=1)
    given, args = {}, {}
    for name, m in arrays.items():
        m = np.ascontiguousarray(m)
        given[f"in_{name}"] = m
        args[name] = nc.dram_tensor(f"in_{name}", m.shape, mybir.dt.from_np(m.dtype), kind="ExternalInput").ap()
    args["out"] = nc.dram_tensor("out_rows", (NPAD + P, FEAT), F32, kind="ExternalOutput").ap()
    gnn_moe_kernel(nc, **args)
    result = run_bass_kernel_spmd(nc, [given], core_ids=[0]).results[0]["out_rows"]
    return result[:NODES]
```

```python
from contextlib import ExitStack

import numpy as np

import concourse.bass as bass
from concourse import mybir

ALU = mybir.AluOpType
ACT = mybir.ActivationFunctionType
F32 = mybir.dt.float32
F32R = mybir.dt.float32r
I32 = mybir.dt.int32
AX_X = mybir.AxisListType.X

P = 128
NODES, FEAT, EDGES = 3125, 256, 50000
MUL, NB, RN, NUM_NEIGH = 64, 8, 64, 16.0
HID, EXPERTS = 1024, 8
EPS = 1e-5

NT = -(-NODES // P)
NPAD = NT * P
GROUP = 5
NG = NT // GROUP
C = 4
STEP = C * P
T = -(-EDGES // STEP)
EPAD = T * STEP
HALF = P // 2
TOK = 256
SUB = TOK // P
LEAST = 3
TILES = 2 * NPAD // TOK + 2 + LEAST * (EXPERTS - 2)
PIECES = 8
SLOTS = T // 2 * TOK
ROW = FEAT + 2
KC = FEAT // P
FC = HID // P
SH = GROUP * P
SHH = SH // 2
WW = KC * HID + FC * FEAT
assert NG * GROUP == NT and T % 2 == 0 and T // 2 >= TILES + 1

C_S = float(np.float32(np.sin(np.pi / 8.0)))
C_X = float(np.float32(np.cos(np.pi / 8.0)))
INV_M = 1.0 / float(np.sqrt(MUL))
OUT_SCALE = C_X / float(np.sqrt(2 * MUL)) / float(np.sqrt(NUM_NEIGH))
INV_SQRT3 = 1.0 / float(np.sqrt(3.0))


def at(i, n=1):
    return bass.ds(i, n)


def gnn_moe_kernel(nc, x, src_t, dst_t, dst_w, sh_t, ele_t, z_t, w_sc0, w_sc1, w_l0, w_l1, fc0, fc1, w_20, w_21,
                   w_r, w1, b1, w2, b2, out):
    def dram(name, shape, dt=F32):
        return nc.dram_tensor(name, shape, dt, kind="Internal").ap()

    h_tab = dram("h_tab", (NPAD, FEAT))
    ele_split = dram("ele_split", (2 * NB, EPAD))
    span_d = dram("span_d", (T, 2))
    xnew_d = dram("xnew_d", (NPAD, FEAT))
    xn_d = dram("xn_d", (NPAD, FEAT))
    xT_d = dram("xT_d", (2, P, KC, NPAD - SH))
    slots_d = dram("slots_d", (SLOTS, ROW))

    with ExitStack() as whole:
        def keep(name, shape, dt=F32):
            return whole.enter_context(nc.sbuf_tensor(name, shape, dt))

        ident = keep("ident", [P, P])
        ones = keep("ones", [P, P])
        earlier = keep("earlier", [P, P])
        iota_row = keep("iota_row", [P, P])
        counts_i = keep("counts_i", [1, 2 * EXPERTS], I32)
        pos_i = keep("pos_i", [P, NT, 2], I32)
        meta_i = keep("meta_i", [P, NT, 2, 2], I32)
        logits = keep("logits", [P, NT, EXPERTS])

        raw = keep("x_raw", [P, WW])
        whi0 = keep("x_whi0", [P, WW], F32R)
        wlo0 = keep("x_wlo0", [P, WW], F32R)
        b1_sb = keep("x_b1", [P, EXPERTS + 1, FC])
        cols_hi = keep("cols_hi", [P, KC, SH], F32R)
        cols_lo = keep("cols_lo", [P, KC, SH], F32R)
        w_in, whi_done, wlo_done = (whole.enter_context(nc.semaphore(n)) for n in ("w_in", "whi_done", "wlo_done"))

        with ExitStack() as graph:
            def gkeep(name, shape, dt=F32):
                return graph.enter_context(nc.sbuf_tensor(name, shape, dt))

            s_sb = gkeep("s_sb", [P, NT, FEAT])
            y_sb = gkeep("y_sb", [P, NT + 1, 8, MUL])
            zo = gkeep("zo", [P, NT])
            with ExitStack() as edges:
                def ekeep(name, shape, dt=F32):
                    return edges.enter_context(nc.sbuf_tensor(name, shape, dt))

                rounds_i = ekeep("rounds_i", [1, 1], I32)
                first_block = ekeep("first_block", [P, T])
                src_sb = ekeep("src_sb", [P, T, C], I32)
                dst_all = ekeep("dst_all", [P, T, C])
                residue = ekeep("residue", [P, T, C])
                sh_sb = ekeep("sh_sb", [P, T, 4 * C])
                w0 = ekeep("w0", [MUL, P], F32R)
                w1hi = ekeep("w1hi", [P, 4 * MUL], F32R)
                w1lo = ekeep("w1lo", [P, 4 * MUL], F32R)
                node_block(nc, locals())
                edge_block(nc, locals())
            update_block(nc, locals())
        expert_blocks(nc, locals())


def chain_of(eng, sem):
    done = [0]

    def link(ins):
        done[0] += 1
        ins.then_inc(sem, 1)
        eng.wait_ge(sem, done[0])

    return link


def node_block(nc, v):
    x, z_t, dst_w, ele_t = v["x"], v["z_t"], v["dst_w"], v["ele_t"]
    s_sb, zo = v["s_sb"], v["zo"]
    ident, ones, earlier, iota_row = v["ident"], v["ones"], v["earlier"], v["iota_row"]
    h_tab, ele_split, span_d = v["h_tab"], v["ele_split"], v["span_d"]
    first_block, rounds_i, y_sb = v["first_block"], v["rounds_i"], v["y_sb"]
    src_sb, dst_all, residue, sh_sb = v["src_sb"], v["dst_all"], v["residue"], v["sh_sb"]
    w0, w1hi, w1lo = v["w0"], v["w1hi"], v["w1lo"]
    raw, whi0, wlo0 = v["raw"], v["whi0"], v["wlo0"]
    EW = NB * EPAD // P
    assert EW <= WW and NG % 2 == 1

    with ExitStack() as ctx:
        def sb(name, shape, dt=F32):
            return ctx.enter_context(nc.sbuf_tensor(name, shape, dt))

        def pb(name):
            return ctx.enter_context(nc.psum_tensor(name, [P, 512], F32))

        def sem(name):
            return ctx.enter_context(nc.semaphore(name))

        x_sb = sb("x_sb", [P, NT, FEAT])
        z_sb = sb("z_sb", [P, NT])
        zi = sb("zi", [P, NT])
        zs = sb("zs", [P, NT])
        wpair = sb("wpair", [P, 2, 4 * MUL])
        stats = sb("stats", [P, GROUP, 6])
        mv = sb("mv", [P, GROUP, 2])
        root = sb("root", [P, GROUP])
        rstd = sb("rstd", [P, GROUP])
        eps = sb("eps", [P, 1])
        warm = sb("warm", [P, 1])
        xn = sb("xn", [P, GROUP, FEAT])
        xT = sb("xT", [P, 2, FEAT])
        dst_i = sb("dst_i", [T, STEP], I32)
        dst_f = sb("dst_f", [T, STEP])
        span = sb("span", [T, 2])
        span_all = sb("span_all", [P, T, 2])
        low_i = sb("low_i", [P, T], I32)
        far = sb("far", [P, T])
        far_i = sb("far_i", [P, T], I32)
        far_f = sb("far_f", [P, T])
        rounds = sb("rounds", [P, 1])
        dst_ti = sb("dst_ti", [P, T, C], I32)
        residue_i = sb("residue_i", [P, T, C], I32)
        w0raw = sb("w0raw", [MUL, P])
        w0hi = sb("w0hi", [MUL, P], F32R)
        w1raw = sb("w1raw", [P, 4 * MUL])
        e_raw, e_hi, e_lo = raw[:, 0:EW], whi0[:, 0:EW], wlo0[:, 0:EW]
        psT = [pb(f"node_psT{i}") for i in range(2)]
        psH = [pb(f"node_psH{i}") for i in range(2)]

        z_in, w_in, dst_in, e_in, tab_in = sem("z_in"), sem("nw_in"), sem("dst_in"), sem("e_in"), sem("tab_in")
        fc_in = sem("fc_in")
        x_in = [sem(f"x_in{g}") for g in range(NG)]
        span_out, span_in, e_out = sem("span_out"), sem("span_in"), sem("e_out")
        h_out = sem("h_out")
        consts, wzero, zscaled, fczero = sem("consts"), sem("wzero"), sem("zscaled"), sem("fczero")
        pool_step, dve_step = sem("pool_step"), sem("dve_step")
        e_split_hi, e_split_lo, span_done = sem("e_split_hi"), sem("e_split_lo"), sem("span_done")
        passed = sem("passed")
        x_ready, stats_done, aggr_done, root_done = sem("x_ready"), sem("stats_done"), sem("aggr_done"), sem("root_done")
        rstd_done = sem("rstd_done")
        xn_ready, turned, xT_ready = sem("xn_ready"), sem("turned"), sem("xT_ready")
        mixed, h_ready, s_ready = sem("mixed"), sem("h_ready"), sem("s_ready")
        block = ctx.enter_context(nc.Block())


        @block.sync
        def _(sp):
            sp.dma_start(z_sb[:], z_t).then_inc(z_in, 16)
            for g in range(NG):
                if g == 1:
                    sp.dma_start(dst_i[:], dst_w).then_inc(dst_in, 16)
                    sp.wait_ge(x_in[0], 16)
                    sp.sem_inc(x_ready, 1)
                    sp.wait_ge(w_in, 16 * 8)
                sp.dma_start(x_sb[:, GROUP * g:GROUP * (g + 1), :],
                             x.rearrange("(t p) f -> p t f", p=P)[:, GROUP * g:GROUP * (g + 1), :]
                             ).then_inc(x_in[g], 16)
            sp.dma_start(e_raw, ele_t.rearrange("b e -> (b e)").rearrange("(p w) -> p w", p=P)).then_inc(e_in, 16)
            for dst, src in ((src_sb, v["src_t"]), (dst_ti, v["dst_t"]), (sh_sb, v["sh_t"])):
                sp.dma_start(dst[:].rearrange("p t c -> p (t c)"), src).then_inc(tab_in, 16)
            sp.wait_ge(fczero, 1)
            sp.wait_ge(pool_step, 2)
            for half in range(2):
                sp.dma_start(w0raw[32 * half:32 * half + 2 * NB, :], v["fc0"]).then_inc(fc_in, 16)
            sp.dma_start(w1raw[:], v["fc1"]).then_inc(fc_in, 16)
            sp.wait_ge(span_done, 1)
            sp.dma_start(span_d, span[:]).then_inc(span_out, 16)
            for g in range(1, NG):
                sp.wait_ge(x_in[g], 16)
                sp.sem_inc(x_ready, 1)
            sp.wait_ge(span_out, 16)
            sp.dma_start(span_all[:], span_d.rearrange("t (o c) -> o t c", o=1).to_broadcast([P, T, 2])
                         ).then_inc(span_in, 16)
            flat = ele_split.rearrange("r e -> (r e)").rearrange("(h p w) -> h p w", h=2, p=P)
            sp.wait_ge(e_split_hi, 1)
            sp.dma_start(flat[0], e_hi.bitcast(F32)).then_inc(e_out, 16)
            sp.wait_ge(e_split_lo, 1)
            sp.dma_start(flat[1], e_lo.bitcast(F32)).then_inc(e_out, 16)
            sp.wait_ge(e_out, 32)

        @block.gpsimd
        def _(pool):
            link = chain_of(pool, pool_step)
            link(pool.memset(wpair[:], 0.0))
            pool.sem_inc(wzero, 1)
            link(pool.memset(w0raw[:], 0.0))
            pool.sem_inc(fczero, 1)
            link(pool.memset(eps[:], EPS))
            link(pool.memset(ident[:], 0.0))
            link(pool.affine_select(out=ident[:], in_=ident[:], compare_op=ALU.not_equal, fill=1.0, base=0,
                                    pattern=[[-1, P]], channel_multiplier=1))
            pool.sem_inc(consts, 1)
            link(pool.memset(ones[:], 1.0))
            link(pool.affine_select(out=earlier[:], in_=ones[:], compare_op=ALU.is_ge, fill=0.0, base=-1,
                                    pattern=[[1, P]], channel_multiplier=-1))
            link(pool.iota(iota_row[:], [[1, P]], base=0, channel_multiplier=0,
                           allow_small_or_imprecise_dtypes=True))
            link(pool.memset(y_sb[:], 0.0))
            pool.wait_ge(e_in, 16)
            pool.tensor_copy(e_hi, e_raw).then_inc(e_split_hi, 1)
            pool.wait_ge(e_split_hi, 1)
            pool.tensor_tensor(e_lo, e_raw, e_hi.bitcast(F32), ALU.subtract).then_inc(e_split_lo, 1)
            pool.wait_ge(fc_in, 16 * 3)
            link(pool.tensor_copy(w0hi[:], w0raw[:]))
            pool.tensor_copy(w0[0:32, :], w0raw[0:32, :])
            link(pool.tensor_tensor(w0[32:64, :], w0raw[32:64, :], w0hi[32:64, :].bitcast(F32), ALU.subtract))
            link(pool.tensor_scalar(w1raw[:], w1raw[:], 1.0 / float(np.sqrt(RN)), None, ALU.mult))
            link(pool.tensor_copy(w1hi[:], w1raw[:]))
            link(pool.tensor_tensor(w1lo[:], w1raw[:], w1hi[:].bitcast(F32), ALU.subtract))
            link(pool.memset(v["cols_lo"][:].bitcast(F32), 0.0))

        @block.vector
        def _(dve):
            link = chain_of(dve, dve_step)

            def normalize(g, tile):
                dve.wait_ge(x_ready, g + 1)
                dve.sem_inc(passed, 1)
                for j in range(GROUP):
                    ins = nc.vector.bn_stats(stats[:, j, :], x_sb[:, at(tile + j), :].rearrange("p o f -> p (o f)"))
                ins.then_inc(stats_done, 1)
                dve.wait_ge(stats_done, g + 1)
                dve.sem_inc(passed, 1)
                for j in range(GROUP):
                    ins = nc.vector.bn_aggr(mv[:, j, :], stats[:, j, :])
                ins.then_inc(aggr_done, 1)
                dve.wait_ge(root_done, g + 1)
                nc.vector.reciprocal(rstd[:], root[:]).then_inc(rstd_done, 1)
                dve.wait_ge(rstd_done, g + 1)
                for j in range(GROUP):
                    dve.wait_ge(turned, g * GROUP + j + 1)
                    row = x_sb[:, at(tile + j), :].rearrange("p o f -> p (o f)")
                    nc.vector.tensor_scalar(xn[:, j, 0:MUL], row[:, 0:MUL], mv[:, j, 0:1], rstd[:, j:j + 1],
                                            ALU.subtract, ALU.mult)
                    nc.vector.tensor_scalar(xn[:, j, MUL:].rearrange("p (c u) -> p u c", c=3),
                                            row[:, MUL:].rearrange("p (u c) -> p u c", c=3),
                                            mv[:, j, 0:1], rstd[:, j:j + 1],
                                            ALU.subtract, ALU.mult).then_inc(xn_ready, 1)

            normalize(0, 0)
            dve.wait_ge(z_in, 16)
            nc.vector.tensor_scalar(zi[:], z_sb[:], INV_M, None, ALU.mult)
            nc.vector.tensor_scalar(zs[:], z_sb[:], INV_M * C_S, None, ALU.mult)
            nc.vector.tensor_scalar(zo[:], z_sb[:], OUT_SCALE, None, ALU.mult).then_inc(zscaled, 1)
            dve.wait_ge(dst_in, 16)
            link(nc.vector.tensor_copy(dst_f[:], dst_i[:]))
            nc.vector.tensor_reduce(span[:, 0:1], dst_f[:], AX_X, ALU.min)
            nc.vector.tensor_reduce(span[:, 1:2], dst_f[:], AX_X, ALU.max).then_inc(span_done, 1)
            with dve.Fori(0, NG - 1) as h:
                normalize(h + 1, (h + 1) * GROUP)
            dve.wait_ge(tab_in, 48)
            link(nc.vector.tensor_copy(dst_all[:], dst_ti[:]))
            link(nc.vector.tensor_single_scalar(residue_i[:], dst_ti[:], P - 1, ALU.bitwise_and))
            link(nc.vector.tensor_copy(residue[:], residue_i[:]))
            dve.wait_ge(span_in, 16)
            link(nc.vector.tensor_copy(low_i[:], span_all[:, :, 0]))
            link(nc.vector.tensor_single_scalar(low_i[:], low_i[:], 6, ALU.logical_shift_right))
            link(nc.vector.tensor_copy(first_block[:], low_i[:]))
            link(nc.vector.scalar_tensor_tensor(out=far[:], in0=first_block[:], scalar=-float(HALF),
                                                in1=span_all[:, :, 1], op0=ALU.mult, op1=ALU.add))
            link(nc.vector.tensor_copy(far_i[:], far[:]))
            link(nc.vector.tensor_single_scalar(far_i[:], far_i[:], 7, ALU.logical_shift_right))
            link(nc.vector.tensor_copy(far_f[:], far_i[:]))
            link(nc.vector.tensor_reduce(rounds[:], far_f[:], AX_X, ALU.max))
            link(nc.vector.tensor_scalar(rounds[:], rounds[:], 1.0, None, ALU.add))
            link(nc.vector.tensor_copy(rounds_i[:], rounds[0:1, :]))

        @block.scalar
        def _(act):
            act.wait_ge(wzero, 1)
            act.wait_ge(pool_step, 3)
            nc.scalar.activation(warm[:], eps[:], ACT.Sqrt)
            w_l0, w_l1, w_sc0, w_sc1 = v["w_l0"], v["w_l1"], v["w_sc0"], v["w_sc1"]
            for pair in range(2):
                for half, (lin, own) in enumerate([(w_l0, w_sc0), (w_l1, w_sc1)] if pair == 0
                                                  else [(w_l1, w_sc1)] * 2):
                    rows = slice(MUL * half, MUL * half + MUL)
                    act.dma_start(wpair[rows, pair, MUL * half:MUL * half + MUL], lin).then_inc(w_in, 16)
                    act.dma_start(wpair[rows, pair, 2 * MUL + MUL * half:3 * MUL + MUL * half], own
                                  ).then_inc(w_in, 16)

            def square_root(g):
                act.wait_ge(aggr_done, g + 1)
                nc.scalar.activation(root[:], mv[:, :, 1], ACT.Sqrt, bias=eps[:]).then_inc(root_done, 1)

            def copy_columns(g, q, j):
                t, i = g * GROUP + j, (q + j) % 2
                act.wait_ge(turned, t + 1 + GROUP)
                act.wait_ge(mixed, t + 1)
                nc.scalar.activation(xT[:, i, :], psT[i][:, 0:FEAT], ACT.Copy).then_inc(xT_ready, 1)

            def copy_rows(g, q, j):
                t, i = g * GROUP + j, (q + j) % 2
                act.wait_ge(mixed, t + 1 + 2)
                pair = psH[i][:, :].rearrange("p (a k w) -> p a k w", a=2, k=2)
                nc.scalar.activation(x_sb[:, at(t), :].rearrange("p o (a w) -> p (o a) w", a=2), pair[:, :, 0, :],
                                     ACT.Copy, scale=zi[:, at(t)]).then_inc(h_ready, 1)
                nc.scalar.activation(s_sb[:, at(t), :].rearrange("p o (a w) -> p (o a) w", a=2), pair[:, :, 1, :],
                                     ACT.Copy, scale=zs[:, at(t)]).then_inc(s_ready, 1)

            def group(h, q, more):
                g = h * 2 + q
                for j in range(GROUP):
                    if j + 1 < GROUP:
                        copy_columns(g, q, j + 1)
                    elif more:
                        copy_columns(g + 1, 1 - q, 0)
                    copy_rows(g, q, j)
                    if j == 1 and more:
                        square_root(g + 1)
                first = act.snap(g * GROUP) if more else g * GROUP
                act.wait_ge(h_ready, (g + 1) * GROUP)
                act.dma_start(h_tab.rearrange("(t p) f -> p t f", p=P)[:, at(first, GROUP), :],
                              x_sb[:, at(first, GROUP), :]).then_inc(h_out, 16)

            square_root(0)
            act.wait_ge(zscaled, 1)
            act.sem_inc(xT_ready, 2)
            act.sem_inc(s_ready, 2)
            copy_columns(0, 0, 0)
            with act.Fori(0, NG // 2) as h:
                for q in range(2):
                    group(h, q, True)
            group(NG // 2, 0, False)
            act.wait_ge(h_out, 16 * NG)

        @block.tensor
        def _(pe):
            pe.sem_inc(turned, GROUP)
            pe.sem_inc(mixed, 2)
            pe.wait_ge(consts, 1)
            pe.wait_ge(pool_step, 5)
            pe.wait_ge(w_in, 16 * 8)

            def turn(g, q, j):
                t, i = g * GROUP + j, (q + j) % 2
                pe.wait_ge(xn_ready, t + 1)
                pe.wait_ge(xT_ready, t + 1)
                for a in range(2):
                    ins = nc.tensor.transpose(psT[i][:, P * a:P * a + P], xn[:, j, P * a:P * a + P], ident[:])
                ins.then_inc(turned, 1)

            def mix(g, q, j):
                t, i = g * GROUP + j, (q + j) % 2
                pe.wait_ge(xT_ready, t + 1 + 2)
                pe.wait_ge(s_ready, t + 1)
                for a in range(2):
                    ins = nc.tensor.matmul(psH[i][:, 4 * MUL * a:4 * MUL * (a + 1)],
                                           xT[:, i, P * a:P * a + P], wpair[:, a, :], start=True, stop=True)
                ins.then_inc(mixed, 1)

            def group(g, q, more):
                for j in range(GROUP):
                    if j + 1 < GROUP:
                        turn(g, q, j + 1)
                    elif more:
                        turn(g + 1, 1 - q, 0)
                    mix(g, q, j)

            turn(0, 0, 0)
            with pe.Fori(0, NG // 2) as h:
                for q in range(2):
                    group(h * 2 + q, q, True)
            group(NG - 1, 0, False)


def edge_block(nc, v):
    src_sb, dst_all, residue, sh_sb = v["src_sb"], v["dst_all"], v["residue"], v["sh_sb"]
    w0, w1hi, w1lo, raw, w_in = v["w0"], v["w1hi"], v["w1lo"], v["raw"], v["w_in"]
    iota_row, first_block, rounds_i, y_sb = v["iota_row"], v["first_block"], v["rounds_i"], v["y_sb"]
    h_tab, ele_split, slots_d, out = v["h_tab"], v["ele_split"], v["slots_d"], v["out"]

    with ExitStack() as ctx:
        def sb(name, shape, dt=F32):
            return ctx.enter_context(nc.sbuf_tensor(name, shape, dt))

        def pb(name):
            return ctx.enter_context(nc.psum_tensor(name, [P, 512], F32))

        def sem(name):
            return ctx.enter_context(nc.semaphore(name))

        key = sb("key", [P, T, C])
        outside = sb("outside", [P, T, C])
        window = sb("window", [P, T])
        row_t = sb("row_t", [1, T])
        low_row = sb("low_row", [1, T], I32)
        high_row = sb("high_row", [1, T], I32)
        e_st, hidT = ([t[:].rearrange("p k n -> p (k n)")[0:rows, STEP * i:STEP * (i + 1)] for i in range(2)]
                      for t, rows in ((v["cols_lo"], MUL), (v["cols_hi"], P)))
        src_st = [sb(f"src_st{i}", [P, C], I32) for i in range(2)]
        sh_st = [sb(f"sh_st{i}", [P, 4 * C]) for i in range(2)]
        hid = [sb(f"hid{i}", [P, STEP]) for i in range(2)]
        rows = [sb(f"rows{i}", [P, C, 4, MUL]) for i in range(2)]
        prod = [sb(f"prod{i}", [P, C, 8 * MUL]) for i in range(2)]
        hot = [sb(f"hot{i}", [P, C, P]) for i in range(2)]
        hots = [sb(f"hots{i}", [P, 4 * C, P]) for i in range(2)]
        blank = sb("blank", [P, ROW])
        warm = sb("e_warm", [P, 1])
        psE = pb("psE")
        psW = [[pb(f"psW{i}{k}") for k in range(2)] for i in range(2)]
        psY = [pb(f"psY{i}") for i in range(2)]

        z_out, all_blank = sem("z_out"), sem("all_blank")
        dve_step, pool_step, blank_set = sem("edve_step"), sem("epool_step"), sem("blank_set")
        e_in = [sem(f"ee_in{i}") for i in range(2)]
        row_in = [[sem(f"row_in{i}{c}") for c in range(C)] for i in range(2)]
        hid_done, silu_done, round_done, low_done = sem("hid_done"), sem("silu_done"), sem("round_done"), sem("low_done")
        w_done, prod_done, hot_done, sh_staged = sem("w_done"), sem("prod_done"), sem("hot_done"), sem("sh_staged")
        hots_done, seg_done, y_done, src_staged = sem("hots_done"), sem("seg_done"), sem("y_done"), sem("src_staged")
        gather_turn = sem("gather_turn")
        block = ctx.enter_context(nc.Block())


        @block.sync
        def _(sp):
            sp.wait_ge(blank_set, 1)
            sp.dma_start(out[NPAD:NPAD + P, :], blank[:, 0:FEAT]).then_inc(z_out, 16)
            R = sp.value_load(rounds_i[0:1, 0:1], min_val=1, max_val=NPAD // P)
            with sp.Fori(0, R) as r:
                with sp.Fori(0, T // 2) as k:
                    for p in range(2):
                        t = k * 2 + p
                        first_edge = sp.snap(t * STEP)
                        sp.wait_ge(hid_done, r * T + t + 1)
                        for half in range(2):
                            sp.dma_start(e_st[p][32 * half:32 * half + 2 * NB, :].bitcast(F32),
                                         ele_split[:, at(first_edge, STEP)]).then_inc(e_in[p], 16)
                    first_slot = sp.snap(k * TOK)
                    sp.dma_start(slots_d[at(first_slot, TOK), :].rearrange("(n p) f -> p n f", p=P),
                                 blank[:].unsqueeze(1).to_broadcast([P, SUB, ROW])).then_inc(z_out, 16)
            load_weights(sp, raw, v["w1"], v["w2"], 0, w_in)
            sp.wait_ge(z_out, 16 + R * (16 * (T // 2)))
            sp.sem_inc(all_blank, 1)
            sp.wait_ge(w_in, 32)

        @block.gpsimd
        def _(pool):
            link = chain_of(pool, pool_step)
            link(pool.memset(blank[:], 0.0))
            link(pool.iota(blank[:, FEAT:FEAT + 1].bitcast(I32), [[0, 1]], base=NPAD, channel_multiplier=1))
            pool.sem_inc(blank_set, 1)
            R = pool.value_load(rounds_i[0:1, 0:1], min_val=1, max_val=NPAD // P)
            with pool.Fori(0, R) as r:
                with pool.Fori(0, T // 2) as k:
                    for p in range(2):
                        t = k * 2 + p
                        pool.wait_ge(prod_done, (r * T + t) * C + C)
                        pool.tensor_copy(src_st[p][:], src_sb[:, at(t), :].rearrange("p o c -> p (o c)")
                                         ).then_inc(src_staged, 1)
                        pool.wait_ge(hots_done, r * T + t + 1)
                        pool.tensor_copy(sh_st[p][:], sh_sb[:, at(t), :].rearrange("p o c -> p (o c)")
                                         ).then_inc(sh_staged, 1)
                        pool.wait_ge(src_staged, r * T + t + 1)
                        pool.sem_inc(gather_turn, 1)
                        for c in range(C):
                            pool.indirect_dma_start(
                                out=rows[p][:, c, :, :].rearrange("p a u -> p (a u)"), out_offset=None, in_=h_tab,
                                in_offset=bass.IndirectOffsetOnAxis(ap=src_st[p][:, c:c + 1], axis=0),
                            ).then_inc(row_in[p][c], 16)

        @block.scalar
        def _(act):
            R = act.value_load(rounds_i[0:1, 0:1], min_val=1, max_val=NPAD // P)

            def silu(r, j, p):
                act.wait_ge(hid_done, r * T + j + 1 + 2)
                act.wait_ge(low_done, r * T + j + 1)
                nc.scalar.activation(hid[p][:], psE[:], ACT.Silu, scale=1.0 / float(np.sqrt(NB))).then_inc(silu_done, 1)

            def scale_hot(r, j, p):
                act.wait_ge(sh_staged, r * T + j + 1)
                act.wait_ge(hot_done, r * T + j + 1)
                act.wait_ge(seg_done, r * T + j + 1)
                for c in range(C):
                    for k in range(4):
                        ins = nc.scalar.activation(hots[p][:, 4 * c + k, :], hot[p][:, c, :], ACT.Copy,
                                                   scale=sh_st[p][:, 4 * c + k:4 * c + k + 1])
                ins.then_inc(hots_done, 1)

            nc.scalar.activation(warm[:], iota_row[:, 0:1], ACT.Silu)
            act.sem_inc(silu_done, 1)
            act.sem_inc(hots_done, 2)
            with act.Fori(0, R) as r:
                silu(r, 0, 0)
                silu(r, 1, 1)
                scale_hot(r, 0, 0)
                with act.Fori(0, T // 2 - 1) as k:
                    for p in range(2):
                        silu(r, k * 2 + p + 2, p)
                        scale_hot(r, k * 2 + p + 1, 1 - p)
                scale_hot(r, T - 1, 1)

        @block.vector
        def _(dve):
            link = chain_of(dve, dve_step)
            link(nc.vector.tensor_copy(window[:], first_block[:]))
            setup_links = 1
            dve.sem_inc(low_done, 2)
            dve.sem_inc(prod_done, 2 * C)
            dve.sem_inc(y_done, 2)
            R = dve.value_load(rounds_i[0:1, 0:1], min_val=1, max_val=NPAD // P)

            def one_hot(r, j, p):
                dve.wait_ge(hots_done, r * T + j + 1)
                nc.vector.tensor_tensor(hot[p][:], iota_row[:].unsqueeze(1).to_broadcast([P, C, P]),
                                        key[:, at(j), :].rearrange("p o c -> p (o c)").unsqueeze(2).to_broadcast([P, C, P]),
                                        ALU.is_equal).then_inc(hot_done, 1)

            def high(r, j, p):
                dve.wait_ge(silu_done, r * T + j + 1 + 1)
                dve.wait_ge(w_done, r * T + j + 1)
                nc.vector.tensor_copy(hidT[p], hid[p][:]).then_inc(round_done, 1)

            def low(r, j, p):
                dve.wait_ge(round_done, r * T + j + 1)
                nc.vector.tensor_tensor(hidT[p][MUL:P, :], hid[p][MUL:P, :], hidT[p][MUL:P, :].bitcast(F32),
                                        ALU.subtract).then_inc(low_done, 1)

            def products(r, k, j, p):
                dve.wait_ge(w_done, r * T + j + 1 + 2)
                dve.wait_ge(seg_done, r * T + j + 1)
                for c in range(C):
                    dve.wait_ge(row_in[p][c], 16 * (r * (T // 2) + k + 1))
                    w = psW[p][c // 2][:, 256 * (c % 2):256 * (c % 2) + 256].rearrange("p (a u) -> p a u", u=MUL)
                    slots = prod[p][:, c, :].rearrange("p (a u) -> p a u", u=MUL)
                    nc.vector.tensor_tensor(slots[:, 0::7, :], w[:, 0:2, :],
                                            rows[p][:, c, 0:1, :].to_broadcast([P, 2, MUL]), ALU.mult)
                    nc.vector.tensor_tensor(
                        slots[:, 1:7, :].rearrange("p (b k) u -> p b k u", b=2),
                        w[:, 2:4, :].unsqueeze(2).to_broadcast([P, 2, 3, MUL]),
                        rows[p][:, c, 1:4, :].unsqueeze(1).to_broadcast([P, 2, 3, MUL]), ALU.mult
                    ).then_inc(prod_done, 1)

            def add_y(r, j, p):
                low_tile = dve.value_load(low_row[0:1, at(j)], min_val=0, max_val=NT)
                high_tile = dve.value_load(high_row[0:1, at(j)], min_val=0, max_val=NT)
                dve.wait_ge(seg_done, r * T + j + 1 + 2)
                dve.wait_ge(y_done, r * T + j + 2)
                for lo, tile in ((0, low_tile), (HALF, high_tile)):
                    acc = y_sb[lo:lo + HALF, at(tile), :, :].rearrange("p o a u -> p (o a u)")
                    ins = nc.vector.tensor_tensor(acc, acc, psY[p][lo:lo + HALF, :], ALU.add)
                ins.then_inc(y_done, 1)

            with dve.Fori(0, R) as r:
                base = setup_links + r * 12
                n = [0]

                def step(ins):
                    n[0] += 1
                    ins.then_inc(dve_step, 1)
                    dve.wait_ge(dve_step, base + n[0])

                wb = window[:].unsqueeze(2).to_broadcast([P, T, C])
                step(nc.vector.scalar_tensor_tensor(out=key[:], in0=wb, scalar=-float(HALF), in1=dst_all[:],
                                                    op0=ALU.mult, op1=ALU.add))
                step(nc.vector.tensor_scalar(outside[:], key[:], 0.0, 1000.0, ALU.is_lt, ALU.mult))
                step(nc.vector.tensor_scalar(key[:], key[:], float(P), 1000.0, ALU.is_ge, ALU.mult))
                step(nc.vector.tensor_tensor(key[:], key[:], outside[:], ALU.add))
                step(nc.vector.tensor_tensor(key[:], key[:], residue[:], ALU.add))
                step(nc.vector.tensor_scalar(row_t[:], window[0:1, :], 1.0, 2.0 * NT, ALU.add, ALU.min))
                step(nc.vector.tensor_copy(low_row[:], row_t[:]))
                step(nc.vector.tensor_single_scalar(low_row[:], low_row[:], 1, ALU.logical_shift_right))
                step(nc.vector.tensor_scalar(row_t[:], window[0:1, :], 2.0 * NT, None, ALU.min))
                step(nc.vector.tensor_copy(high_row[:], row_t[:]))
                step(nc.vector.tensor_single_scalar(high_row[:], high_row[:], 1, ALU.logical_shift_right))
                step(nc.vector.tensor_scalar(window[:], window[:], 2.0, None, ALU.add))
                high(r, 0, 0)
                one_hot(r, 0, 0)
                low(r, 0, 0)
                high(r, 1, 1)
                one_hot(r, 1, 1)
                low(r, 1, 1)
                products(r, 0, 0, 0)
                high(r, 2, 0)
                one_hot(r, 2, 0)
                low(r, 2, 0)
                products(r, 0, 1, 1)
                with dve.Fori(0, T // 2 - 2) as k:
                    for q in range(2):
                        t = k * 2 + 1 + q
                        add_y(r, t - 1, q)
                        high(r, t + 2, 1 - q)
                        one_hot(r, t + 2, 1 - q)
                        low(r, t + 2, 1 - q)
                        products(r, k + 1, t + 1, q)
                add_y(r, T - 4, 0)
                high(r, T - 1, 1)
                one_hot(r, T - 1, 1)
                low(r, T - 1, 1)
                products(r, T // 2 - 1, T - 2, 0)
                add_y(r, T - 3, 1)
                products(r, T // 2 - 1, T - 1, 1)
                add_y(r, T - 2, 0)
                add_y(r, T - 1, 1)

        @block.tensor
        def _(pe):
            R = pe.value_load(rounds_i[0:1, 0:1], min_val=1, max_val=NPAD // P)
            pe.sem_inc(hid_done, 2)
            pe.sem_inc(w_done, 2)
            pe.sem_inc(seg_done, 2)

            def hidden(r, k, j, p):
                pe.wait_ge(e_in[p], 32 * (r * (T // 2) + k + 1))
                pe.wait_ge(silu_done, r * T + j + 1)
                nc.tensor.matmul(psE[:], w0[:], e_st[p], start=True, stop=True).then_inc(hid_done, 1)

            def radial(r, j, p):
                pe.wait_ge(low_done, r * T + j + 1 + 2)
                pe.wait_ge(prod_done, (r * T + j) * C + C)
                for c in range(C):
                    o = psW[p][c // 2][:, 256 * (c % 2):256 * (c % 2) + 256]
                    nc.tensor.matmul(o, hidT[p][:, P * c:P * c + P], w1hi[:], start=True, stop=False)
                    ins = nc.tensor.matmul(o, hidT[p][:, P * c:P * c + P], w1lo[:], start=False, stop=True)
                ins.then_inc(w_done, 1)

            def segment(r, j, p):
                pe.wait_ge(hots_done, r * T + j + 1 + 2)
                pe.wait_ge(y_done, r * T + j + 1)
                y = psY[p][:, :].rearrange("p (a u) -> p a u", u=MUL)
                for c in range(C):
                    pe.wait_ge(prod_done, (r * T + j) * C + c + 1 + 2 * C)
                    a = prod[p][:, c, :].rearrange("p (a u) -> p a u", u=MUL)
                    ins = nc.tensor.matmul(y[:, 1::2, :], hots[p][:, 4 * c, :], a[:, 4:8, :], start=(c == 0),
                                           stop=(c == C - 1), skip_group_check=True)
                    for k in range(3):
                        ins = nc.tensor.matmul(y[:, 2 * k::6 - 2 * k, :][:, 0:2, :], hots[p][:, 4 * c + k + 1, :],
                                               a[:, 0::k + 1, :][:, 0:2, :], start=False, stop=(c == C - 1),
                                               skip_group_check=True)
                ins.then_inc(seg_done, 1)

            with pe.Fori(0, R) as r:
                hidden(r, 0, 0, 0)
                hidden(r, 0, 1, 1)
                radial(r, 0, 0)
                with pe.Fori(0, T // 2 - 1) as k:
                    for p in range(2):
                        t = k * 2 + p
                        hidden(r, k + 1, t + 2, p)
                        radial(r, t + 1, 1 - p)
                        segment(r, t, p)
                radial(r, T - 1, 1)
                segment(r, T - 2, 0)
                segment(r, T - 1, 1)



def update_block(nc, v):
    s_sb, y_sb, zo, ident, logits = v["s_sb"], v["y_sb"], v["zo"], v["ident"], v["logits"]
    xnew_d, xn_d, xT_d = v["xnew_d"], v["xn_d"], v["xT_d"]
    raw, whi0, wlo0, whi_done, wlo_done = v["raw"], v["whi0"], v["wlo0"], v["whi_done"], v["wlo_done"]
    WP = WW // (NG - 1)
    assert NG % 2 == 1 and WP * (NG - 1) == WW

    with ExitStack() as ctx:
        def sb(name, shape, dt=F32):
            return ctx.enter_context(nc.sbuf_tensor(name, shape, dt))

        def pb(name):
            return ctx.enter_context(nc.psum_tensor(name, [P, 512], F32))

        def sem(name):
            return ctx.enter_context(nc.semaphore(name))

        w2 = sb("u_w2", [P, 4, MUL])
        wr = sb("u_wr", [P, KC, EXPERTS])
        eps = sb("u_eps", [P, 1])
        warm = sb("u_warm", [P, 1])
        x_sb = sb("u_x", [P, NT, FEAT])
        ys = sb("u_ys", [P, GROUP, 512])
        yT = sb("u_yT", [P, 2, 512])
        gnn = sb("u_gnn", [P, GROUP, FEAT])
        stats = sb("u_stats", [P, GROUP, 6])
        mv = sb("u_mv", [P, GROUP, 2])
        root = sb("u_root", [P, GROUP])
        rstd = sb("u_rstd", [P, GROUP])
        xn = sb("u_xn", [P, GROUP, FEAT])
        xT = sb("u_xT", [P, 2, KC, P])
        scoresT = sb("u_scoresT", [EXPERTS, 2, P])
        xhi = [v["cols_hi"], sb("u_xhi1", [P, KC, SH], F32R)]
        xlo = [v["cols_lo"], sb("u_xlo1", [P, KC, SH], F32R)]
        psY = [pb(f"u_psY{i}") for i in range(2)]
        psO = [pb(f"u_psO{i}") for i in range(2)]
        psX = [pb(f"u_psX{i}") for i in range(2)]
        psL = [pb(f"u_psL{i}") for i in range(2)]

        x_in = [sem(f"u_x_in{g}") for g in range(NG)]
        x_ready, whi_part, wparts_done = sem("u_x_ready"), sem("u_whi_part"), sem("u_wparts_done")
        w_in, rows_out, cols_out = sem("u_w_in"), sem("u_rows_out"), sem("u_cols_out")
        w_ready, staged, turned, yT_ready = sem("u_w_ready"), sem("u_staged"), sem("u_turned"), sem("u_yT_ready")
        mixed, gnn_done, x_done, stats_done = sem("u_mixed"), sem("u_gnn_done"), sem("u_x_done"), sem("u_stats_done")
        aggr_go, aggr_done, root_done = sem("u_aggr_go"), sem("u_aggr_done"), sem("u_root_done")
        rstd_done, xn_done, x_turned = sem("u_rstd_done"), sem("u_xn_done"), sem("u_x_turned")
        xT_ready, hi_done, lo_done, scored = sem("u_xT_ready"), sem("u_hi_done"), sem("u_lo_done"), sem("u_scored")
        b1_in = sem("u_b1_in")
        turn_go = sem("u_turn_go")
        scores_ready, scores_turned = sem("u_scores_ready"), sem("u_scores_turned")
        logits_done, rows_free, cols_free = sem("u_logits_done"), sem("u_rows_free"), sem("u_cols_free")
        block = ctx.enter_context(nc.Block())


        @block.sync
        def _(sp):
            for c in range(3):
                sp.dma_start(w2[:, c, :], v["w_21"]).then_inc(w_in, 16)
            sp.dma_start(w2[0:MUL, 3, :], v["w_20"][MUL:2 * MUL, :]).then_inc(w_in, 16)
            sp.dma_start(w2[MUL:P, 3, :], v["w_20"][0:MUL, :]).then_inc(w_in, 16)
            sp.dma_start(wr[:], v["w_r"].rearrange("(k p) e -> p k e", p=P)).then_inc(w_in, 16)
            sp.dma_start(v["b1_sb"][:].rearrange("p e f -> p (e f)"), v["b1"]).then_inc(b1_in, 16)
            for g in range(NG):
                sp.dma_start(x_sb[:, GROUP * g:GROUP * (g + 1), :],
                             v["x"].rearrange("(t p) f -> p t f", p=P)[:, GROUP * g:GROUP * (g + 1), :]
                             ).then_inc(x_in[g], 16)
            sp.sem_inc(rows_free, 1)
            sp.sem_inc(cols_free, 2)
            for g in range(NG):
                sp.wait_ge(x_in[g], 16)
                sp.sem_inc(x_ready, 1)

            def store_rows(g, first):
                sp.wait_ge(xn_done, (g + 1) * GROUP)
                for src, dst in ((x_sb[:, at(first, GROUP), :], xnew_d), (xn[:], xn_d)):
                    sp.dma_start(dst.rearrange("(t p) f -> p t f", p=P)[:, at(first, GROUP), :], src
                                 ).then_inc(rows_out, 16)
                sp.wait_ge(rows_out, 32 * (g + 1))
                sp.sem_inc(rows_free, 1)

            def store_cols(g, q, first_col):
                sp.wait_ge(lo_done, (g + 1) * GROUP + 2)
                for h, part in enumerate((xhi[q], xlo[q])):
                    sp.dma_start(xT_d[h, :, :, at(first_col, SH)], part[:].bitcast(F32)).then_inc(cols_out, 16)
                sp.wait_ge(cols_out, 32 * (g + 1))
                sp.sem_inc(cols_free, 1)

            store_rows(0, 0)
            with sp.Fori(0, NG // 2) as h:
                for q in range(2):
                    first = sp.snap((h * 2 + q + 1) * GROUP)
                    first_col = sp.snap((h * 2 + q) * SH)
                    store_cols(h * 2 + q, q, first_col)
                    store_rows(h * 2 + q + 1, first)
            sp.wait_ge(b1_in, 16)

        @block.gpsimd
        def _(pool):
            with pool.Fori(0, NG) as g:
                for j in range(GROUP):
                    pool.wait_ge(turned, g * GROUP + j + 1)
                    pool.tensor_copy(ys[:, j, :], y_sb[:, at(g * GROUP + j), :, :].rearrange("p o a u -> p (o a u)")
                                     ).then_inc(staged, 1)

        @block.vector
        def _(dve):
            nc.vector.memset(eps[:], EPS)
            dve.wait_ge(w_in, 16 * 6)
            nc.vector.tensor_scalar(w2[0:MUL, 3, :], w2[0:MUL, 3, :], INV_SQRT3, None, ALU.mult).then_inc(w_ready, 1)
            dve.sem_inc(gnn_done, 2)
            dve.sem_inc(lo_done, 2)

            def graph_result(g, q, j):
                t = g * GROUP + j
                dve.wait_ge(mixed, t + 1 + 2)
                nc.vector.scalar_tensor_tensor(
                    out=gnn[:, j, :], in0=psO[(q + j) % 2][:, 0:FEAT], scalar=zo[:, at(t)],
                    in1=s_sb[:, at(t), :].rearrange("p o f -> p (o f)"), op0=ALU.mult, op1=ALU.add
                ).then_inc(gnn_done, 1)

            def residual(g, j):
                t = g * GROUP + j
                dve.wait_ge(gnn_done, t + 1 + 2)
                if j == 0:
                    dve.wait_ge(x_ready, g + 1)
                row = x_sb[:, at(t), :].rearrange("p o f -> p (o f)")
                nc.vector.tensor_tensor(row[:, 0:MUL], row[:, 0:MUL], gnn[:, j, 0:MUL], ALU.add)
                cols = row[:, MUL:].rearrange("p (u c) -> p u c", c=3)
                nc.vector.tensor_tensor(cols, cols, gnn[:, j, MUL:].rearrange("p (c u) -> p u c", c=3),
                                        ALU.add).then_inc(x_done, 1)

            def statistics(g, j):
                t = g * GROUP + j
                dve.wait_ge(x_done, t + 1)
                dve.sem_inc(aggr_go, 1)
                nc.vector.bn_stats(stats[:, j, :], x_sb[:, at(t), :].rearrange("p o f -> p (o f)")
                                   ).then_inc(stats_done, 1)

            def normalize(g, first_group):
                dve.wait_ge(stats_done, (g + 1) * GROUP)
                dve.sem_inc(aggr_go, 1)
                for j in range(GROUP):
                    ins = nc.vector.bn_aggr(mv[:, j, :], stats[:, j, :])
                ins.then_inc(aggr_done, 1)
                dve.wait_ge(root_done, g + 1)
                nc.vector.reciprocal(rstd[:], root[:]).then_inc(rstd_done, 1)
                dve.wait_ge(rstd_done, g + 1)
                dve.wait_ge(rows_free, g + 1)
                if not first_group:
                    dve.wait_ge(x_turned, g * GROUP)
                for j in range(GROUP):
                    nc.vector.tensor_scalar(xn[:, j, :], x_sb[:, at(g * GROUP + j), :].rearrange("p o f -> p (o f)"),
                                            mv[:, j, 0:1], rstd[:, j:j + 1], ALU.subtract, ALU.mult
                                            ).then_inc(xn_done, 1)
                if not first_group:
                    dve.wait_ge(whi_part, g)
                    part = at((g - 1) * WP, WP)
                    nc.vector.tensor_tensor(wlo0[:, part], raw[:, part], whi0[:, part].bitcast(F32), ALU.subtract
                                            ).then_inc(wparts_done, 1)

            def low(g, q, j):
                dve.wait_ge(hi_done, g * GROUP + j + 1)
                nc.vector.tensor_tensor(xlo[q][:, :, P * j:P * j + P], xT[:, (q + j) % 2, :, :],
                                        xhi[q][:, :, P * j:P * j + P].bitcast(F32), ALU.subtract).then_inc(lo_done, 1)

            def first_stage(g, q, columns):
                for j in range(GROUP):
                    graph_result(g, q, j)
                    if columns:
                        low(g - 1, 1 - q, j)
                    if j > 0:
                        statistics(g, j - 1)
                    residual(g, j)
                statistics(g, GROUP - 1)
                normalize(g, not columns)

            first_stage(0, 0, False)
            with dve.Fori(0, NG // 2) as h:
                for q in range(2):
                    first_stage(h * 2 + q + 1, 1 - q, True)
            for j in range(GROUP):
                low(NG - 1, 0, j)
            dve.wait_ge(wparts_done, NG - 1)
            dve.sem_inc(wlo_done, 1)

        @block.scalar
        def _(act):
            act.sem_inc(yT_ready, 2)
            act.sem_inc(xT_ready, 2)
            act.sem_inc(logits_done, 2)
            act.sem_inc(scores_ready, 2)
            nc.scalar.activation(warm[:], ident[:, 0:1], ACT.Sqrt)

            def copy_sums(g, q, j):
                t = g * GROUP + j
                act.wait_ge(turned, t + 1 + GROUP)
                act.wait_ge(mixed, t + 1)
                nc.scalar.activation(yT[:, (q + j) % 2, :], psY[(q + j) % 2][:], ACT.Copy).then_inc(yT_ready, 1)

            def copy_columns(g, q, j):
                t, i = g * GROUP + j, (q + j) % 2
                act.wait_ge(x_turned, t + 1)
                act.wait_ge(scored, t + 1)
                act.wait_ge(lo_done, t + 1)
                nc.scalar.activation(xT[:, i, :, :].rearrange("p k n -> p (k n)"), psX[i][:, 0:FEAT],
                                     ACT.Copy).then_inc(xT_ready, 1)
                act.wait_ge(xT_ready, t + 1 + 2)
                if j == 0:
                    act.wait_ge(cols_free, g + 1)
                nc.scalar.activation(xhi[q][:, :, P * j:P * j + P], xT[:, i, :, :], ACT.Copy).then_inc(hi_done, 1)

            def copy_scores(g, q, j):
                t, i = g * GROUP + j, (q + j) % 2
                act.wait_ge(scored, t + 1 + 2)
                act.wait_ge(scores_turned, t + 1)
                nc.scalar.activation(scoresT[:, i, :], psX[i][0:EXPERTS, FEAT:FEAT + P], ACT.Copy
                                     ).then_inc(scores_ready, 1)

            def copy_logits(g, q):
                act.wait_ge(scores_turned, (g + 1) * GROUP + 2)
                nc.scalar.activation(logits[:, at(g * GROUP, GROUP), :].rearrange("p j e -> p (j e)"),
                                     psL[q][:, 0:GROUP * EXPERTS], ACT.Copy).then_inc(logits_done, 1)

            def square_root(g):
                act.wait_ge(aggr_done, g + 1)
                nc.scalar.activation(root[:], mv[:, :, 1], ACT.Sqrt, bias=eps[:]).then_inc(root_done, 1)

            for j in range(GROUP):
                copy_sums(0, 0, j)
            square_root(0)
            act.sem_inc(whi_done, 1)
            with act.Fori(0, NG // 2) as h:
                for q in range(2):
                    b = h * 2 + q
                    copy_sums(b + 1, 1 - q, 0)
                    for j in range(GROUP):
                        if j + 1 < GROUP:
                            copy_sums(b + 1, 1 - q, j + 1)
                        copy_columns(b, q, j)
                        if j > 0:
                            copy_scores(b, q, j - 1)
                    copy_scores(b, q, GROUP - 1)
                    part = at(b * WP, WP)
                    nc.scalar.activation(whi0[:, part], raw[:, part], ACT.Copy).then_inc(whi_part, 1)
                    square_root(b + 1)
                    copy_logits(b, q)
            for j in range(GROUP):
                copy_columns(NG - 1, 0, j)
                if j > 0:
                    copy_scores(NG - 1, 0, j - 1)
            copy_scores(NG - 1, 0, GROUP - 1)
            copy_logits(NG - 1, 0)

        @block.tensor
        def _(pe):
            pe.sem_inc(turned, GROUP)
            pe.sem_inc(mixed, 2)
            pe.sem_inc(scored, 2)
            pe.sem_inc(scores_turned, 2)

            def turn(g, q, j):
                t, i = g * GROUP + j, (q + j) % 2
                pe.wait_ge(staged, t + 1)
                pe.wait_ge(yT_ready, t + 1)
                for c in range(4):
                    ins = nc.tensor.transpose(psY[i][:, P * c:P * c + P], ys[:, j, P * c:P * c + P], ident[:])
                ins.then_inc(turned, 1)

            def mix(g, q, j):
                t, i = g * GROUP + j, (q + j) % 2
                pe.wait_ge(yT_ready, t + 1 + 2)
                pe.wait_ge(gnn_done, t + 1)
                for c in range(4):
                    o = MUL * (c + 1) if c < 3 else 0
                    ins = nc.tensor.matmul(psO[i][:, o:o + MUL], yT[:, i, P * c:P * c + P], w2[:, c, :],
                                           start=True, stop=True)
                ins.then_inc(mixed, 1)

            def turn_x(g, q, j):
                t, i = g * GROUP + j, (q + j) % 2
                pe.wait_ge(xn_done, t + 1)
                pe.wait_ge(scores_ready, t + 1)
                for k in range(KC):
                    ins = nc.tensor.transpose(psX[i][:, P * k:P * k + P], xn[:, j, P * k:P * k + P], ident[:])
                ins.then_inc(x_turned, 1)

            def score(g, q, j):
                t, i = g * GROUP + j, (q + j) % 2
                pe.wait_ge(xT_ready, t + 1 + 2)
                for k in range(KC):
                    ins = nc.tensor.matmul(psX[i][0:EXPERTS, FEAT:FEAT + P], wr[:, k, :], xT[:, i, k, :],
                                           start=(k == 0), stop=(k == KC - 1))
                ins.then_inc(scored, 1)

            def turn_scores(g, q, j):
                t, i = g * GROUP + j, (q + j) % 2
                pe.wait_ge(scores_ready, t + 1 + 2)
                if j == 0:
                    pe.wait_ge(logits_done, g + 1)
                pe.sem_inc(turn_go, 1)
                nc.tensor.transpose(psL[q][:, EXPERTS * j:EXPERTS * (j + 1)], scoresT[:, i, :],
                                    ident[0:EXPERTS, 0:EXPERTS]).then_inc(scores_turned, 1)

            def columns(g, q, j):
                turn_x(g, q, j)
                if j > 0:
                    score(g, q, j - 1)
                if j > 1:
                    turn_scores(g, q, j - 2)

            def last_scores(g, q):
                score(g, q, GROUP - 1)
                turn_scores(g, q, GROUP - 2)
                turn_scores(g, q, GROUP - 1)

            turn(0, 0, 0)
            for j in range(GROUP):
                if j + 1 < GROUP:
                    turn(0, 0, j + 1)
                if j == 0:
                    pe.wait_ge(w_ready, 1)
                mix(0, 0, j)
            with pe.Fori(0, NG // 2) as h:
                for q in range(2):
                    b = h * 2 + q
                    turn(b + 1, 1 - q, 0)
                    for j in range(GROUP):
                        if j + 1 < GROUP:
                            turn(b + 1, 1 - q, j + 1)
                        mix(b + 1, 1 - q, j)
                        columns(b, q, j)
                    last_scores(b, q)
            for j in range(GROUP):
                columns(NG - 1, 0, j)
            last_scores(NG - 1, 0)


def route_steps(nc, v, sb, dve, link, psR, psT):
    logits, pos_i, meta_i, counts_i = v["logits"], v["pos_i"], v["meta_i"], v["counts_i"]
    E = EXPERTS
    TALL = [P, NT, E]
    falling, token_i, shifted, expd, chosen = (v[k] for k in ("falling", "token_i", "shifted", "expd", "chosen"))
    top = sb("r_top", [P, NT])
    total = sb("r_total", [P, NT])
    inverse = sb("r_inverse", [P, NT])
    gate = sb("r_gate", TALL)
    rest = sb("r_rest", TALL)
    best = [sb(f"r_best{k}", [P, NT]) for k in range(2)]
    same = sb("r_same", TALL)
    pick = sb("r_pick", [P, NT])
    hot = [sb(f"r_hot{k}", TALL) for k in range(2)]
    rank = sb("r_rank", TALL)
    per_tile = sb("r_per_tile", TALL)
    running = [sb(f"r_running{k}", TALL) for k in range(2)]
    slot = sb("r_slot", TALL)
    mine = sb("r_mine", TALL)
    need_i = sb("r_need_i", [P, E], I32)
    need = sb("r_need", [P, E])
    need_f = sb("r_need_f", [P, E])
    ends = [sb(f"r_ends{k}", [P, E]) for k in range(2)]
    start = sb("r_start", [P, E])
    pos = sb("r_pos", [P, NT])
    DOUBLINGS = (NT - 1).bit_length()
    run = running[DOUBLINGS % 2]

    def wide(a):
        return a.unsqueeze(2).to_broadcast(TALL)

    def shift():
        link(nc.vector.tensor_reduce(top[:], logits[:], AX_X, ALU.max))
        link(nc.vector.tensor_tensor(shifted[:], logits[:], wide(top[:]), ALU.subtract))
        dve.sem_inc(v["shift_done"], 1)

    def softmax():
        dve.wait_ge(v["exp_done"], 1)
        link(nc.vector.tensor_reduce(total[:], expd[:], AX_X, ALU.add))
        link(nc.vector.reciprocal(inverse[:], total[:]))
        link(nc.vector.tensor_tensor(gate[:], expd[:], wide(inverse[:]), ALU.mult))

    def best_value(k):
        values = rest if k else gate
        link(nc.vector.tensor_reduce(best[k][:], values[:], AX_X, ALU.max))
        link(nc.vector.tensor_tensor(same[:], values[:], wide(best[k][:]), ALU.is_equal))
        link(nc.vector.tensor_tensor(same[:], same[:], falling[:].unsqueeze(1).to_broadcast(TALL), ALU.mult))

    def best_expert(k):
        link(nc.vector.tensor_reduce(pick[:], same[:], AX_X, ALU.max))
        link(nc.vector.tensor_tensor(hot[k][:], falling[:].unsqueeze(1).to_broadcast(TALL), wide(pick[:]), ALU.is_equal))
        if k == 0:
            link(nc.vector.scalar_tensor_tensor(out=rest[:], in0=hot[0][:], scalar=-4.0, in1=gate[:],
                                                op0=ALU.mult, op1=ALU.add))

    def choose():
        link(nc.vector.tensor_tensor(chosen[:], hot[0][:], hot[1][:], ALU.add))
        dve.sem_inc(v["chosen_done"], 1)
        link(nc.vector.tensor_tensor(total[:], best[0][:], best[1][:], ALU.add))
        link(nc.vector.reciprocal(inverse[:], total[:]))

    def gates():
        for k in range(2):
            nc.vector.tensor_tensor(meta_i[:, :, k, 1].bitcast(F32), best[k][:], inverse[:], ALU.mult)
            link(nc.vector.tensor_copy(meta_i[:, :, k, 0], token_i[:]))

    def counts():
        dve.wait_ge(v["counted"], 1)
        nc.vector.tensor_copy(rank[:].rearrange("p t e -> p (t e)"), psR[:, 0:NT * E])
        link(nc.vector.tensor_copy(per_tile[:].rearrange("p t e -> p (t e)"), psT[:, 0:NT * E]))
        link(nc.vector.tensor_copy(running[0][:], per_tile[:]))

    def doubling(n):
        old, new, d = running[n % 2], running[1 - n % 2], 2 ** n
        nc.vector.tensor_copy(new[:, 0:d, :], old[:, 0:d, :])
        link(nc.vector.tensor_tensor(new[:, d:, :], old[:, d:, :], old[:, 0:NT - d, :], ALU.add))

    def tiles_needed():
        link(nc.vector.tensor_scalar(need[:], run[:, NT - 1, :], float(TOK - 1), None, ALU.add))
        link(nc.vector.tensor_copy(need_i[:], need[:]))
        link(nc.vector.tensor_single_scalar(need_i[:], need_i[:], TOK.bit_length() - 1, ALU.logical_shift_right))
        link(nc.vector.tensor_copy(need_f[:], need_i[:]))
        link(nc.vector.tensor_scalar(need[:], need_f[:], float(LEAST), None, ALU.max))

    def first_tiles():
        link(nc.vector.tensor_copy(ends[0][:], need[:]))
        at_, d = 0, 1
        while d < E:
            a, b = ends[at_], ends[1 - at_]
            nc.vector.tensor_copy(b[:, 0:d], a[:, 0:d])
            link(nc.vector.tensor_tensor(b[:, d:], a[:, d:], a[:, 0:E - d], ALU.add))
            at_, d = 1 - at_, 2 * d
        link(nc.vector.tensor_tensor(start[:], ends[at_][:], need[:], ALU.subtract))
        nc.vector.tensor_copy(counts_i[:, 0:E], need[0:1, :])
        link(nc.vector.tensor_copy(counts_i[:, E:2 * E], start[0:1, :]))

    def slots():
        link(nc.vector.tensor_tensor(slot[:], run[:], per_tile[:], ALU.subtract))
        link(nc.vector.tensor_tensor(slot[:], slot[:], rank[:], ALU.add))
        link(nc.vector.scalar_tensor_tensor(out=slot[:], in0=start[:].unsqueeze(1).to_broadcast(TALL),
                                            scalar=float(TOK), in1=slot[:], op0=ALU.mult, op1=ALU.add))

    def place():
        for k in range(2):
            link(nc.vector.tensor_tensor(mine[:], slot[:], hot[k][:], ALU.mult))
            link(nc.vector.tensor_reduce(pos[:], mine[:], AX_X, ALU.add))
            link(nc.vector.tensor_copy(pos_i[:, :, k], pos[:]))
        dve.sem_inc(v["placed"], 1)

    return (shift, softmax, best_value, best_expert, choose, gates, counts, doubling, tiles_needed, first_tiles,
            slots, place, DOUBLINGS)


def load_weights(eng, raw, w1, w2, e, sem):
    eng.dma_start(raw[:, 0:KC * HID].rearrange("p (k f) -> p k f", k=KC),
                  w1[at(e)].rearrange("o (k p) f -> p (o k) f", p=P)).then_inc(sem, 16)
    eng.dma_start(raw[:, KC * HID:].rearrange("p (k f) -> p k f", k=FC),
                  w2[at(e)].rearrange("o (k p) f -> p (o k) f", p=P)).then_inc(sem, 16)


def expert_blocks(nc, v):
    with ExitStack() as ctx:
        def sb(name, shape, dt=F32):
            return ctx.enter_context(nc.sbuf_tensor(name, shape, dt))

        whi = [v["whi0"], sb("x_whi1", [P, WW], F32R)]
        wlo = [v["wlo0"], sb("x_wlo1", [P, WW], F32R)]
        b2_sb = sb("x_b2", [P, EXPERTS + 1, FEAT])
        o_out = ctx.enter_context(nc.semaphore("o_out"))
        slot_in = ctx.enter_context(nc.semaphore("slot_in"))
        slot_tile = sb("x_slot_tile", [P, SUB, ROW])
        shared = dict(v, o_out=o_out, slot_in=slot_in, slot_tile=slot_tile, whi=whi, wlo=wlo, b2_sb=b2_sb)
        shared_block(nc, shared)
        routed_block(nc, shared)


def w1_part(w, k, f):
    return w[:, k * HID + P * f:k * HID + P * f + P]


def w2_part(w, f):
    return w[:, KC * HID + FEAT * f:KC * HID + FEAT * f + FEAT]


def up_product(nc, ps, whi, wlo, xhi, xlo, f):
    terms = [(w, x, k) for k in range(KC) for w, x in ((whi, xhi), (whi, xlo), (wlo, xhi))]
    for n, (w, x, k) in enumerate(terms):
        ins = nc.tensor.matmul(ps, w1_part(w, k, f), x(k), start=(n == 0), stop=(n == len(terms) - 1))
    return ins


def down_product(nc, ps, hhi, hlo, whi, wlo, f):
    for n, (h, w) in enumerate(((hhi, whi), (hhi, wlo), (hlo, whi))):
        ins = nc.tensor.matmul(ps, h, w2_part(w, f), start=(f == 0 and n == 0), stop=(f == FC - 1 and n == 2))
    return ins


def shared_block(nc, v):
    raw, whi, wlo, b1_sb, b2_sb = v["raw"], v["whi"], v["wlo"], v["b1_sb"], v["b2_sb"]
    w1, w2, out, xT_d, xnew_d, xn_d, slots_d = (v[k] for k in ("w1", "w2", "out", "xT_d", "xnew_d", "xn_d", "slots_d"))
    pos_i, meta_i = v["pos_i"], v["meta_i"]

    with ExitStack() as ctx:
        def sb(name, shape, dt=F32):
            return ctx.enter_context(nc.sbuf_tensor(name, shape, dt))

        def pb(name):
            return ctx.enter_context(nc.psum_tensor(name, [P, 512], F32))

        def sem(name):
            return ctx.enter_context(nc.semaphore(name))

        xhi, xlo = v["cols_hi"], v["cols_lo"]
        xnew = sb("s_xnew", [P, GROUP, FEAT])
        hf = [sb(f"s_hf{i}", [P, SHH]) for i in range(4)]
        hhi = sb("s_hhi", [P, FC, SH], F32R)
        hlo = sb("s_hlo", [P, FC, SH], F32R)
        biased = sb("s_biased", [P, 2, FEAT])
        ob = sb("s_ob", [P, GROUP, FEAT])
        row = [[sb(f"s_row{j}{k}", [P, ROW]) for k in range(2)] for j in range(GROUP)]
        pos_st = [sb(f"s_pos{j}", [P, 2], I32) for j in range(GROUP)]
        TALL = [P, NT, EXPERTS]
        falling = sb("r_falling", [P, EXPERTS])
        token_i = sb("r_token", [P, NT], I32)
        shifted = sb("r_shifted", TALL)
        warm = sb("s_warm", [P, 2])
        expd = sb("r_expd", TALL)
        chosen = sb("r_chosen", TALL)
        psA = [pb(f"s_psA{i}") for i in range(4)]
        psB = [pb(f"s_psB{i}") for i in range(2)]
        psR, psT = pb("r_psR"), pb("r_psT")

        w_in, whi_done, wlo_done = v["w_in"], v["whi_done"], v["wlo_done"]
        b_in, xT_in, xnew_in = sem("s_b_in"), sem("s_xT_in"), sem("s_xnew_in")
        o_out = v["o_out"]
        row_in = [sem(f"s_row_in{j}") for j in range(GROUP)]
        sent = [sem(f"s_sent{j}") for j in range(GROUP)]
        row_free, ob_free, row_go, pos_staged = sem("s_row_free"), sem("s_ob_free"), sem("s_row_go"), sem("s_pos_staged")
        up_done, gelu_done, hhi_done, hlo_done = sem("s_up_done"), sem("s_gelu_done"), sem("s_hhi_done"), sem("s_hlo_done")
        down_done, biased_done, ob_done = sem("s_down_done"), sem("s_biased_done"), sem("s_ob_done")
        whi_part, wlo_part = sem("s_whi_part"), sem("s_wlo_part")
        r_consts, r_step, shift_done, exp_done = sem("r_consts"), sem("r_step"), sem("r_shift_done"), sem("r_exp_done")
        chosen_done, counted, placed = sem("r_chosen_done"), sem("r_counted"), sem("r_placed")
        router = dict(v, falling=falling, token_i=token_i, shifted=shifted, expd=expd, chosen=chosen,
                      shift_done=shift_done, exp_done=exp_done, chosen_done=chosen_done, counted=counted, placed=placed)
        block = ctx.enter_context(nc.Block())
        WP = WW // (NG - 1)
        UP = 2 * FC


        @block.sync
        def _(sp):
            def load_rows(turn, group):
                first = [sp.snap((group * GROUP + j) * P) if turn is not None else (group * GROUP + j) * P
                         for j in range(GROUP)]
                for j in range(GROUP):
                    if turn is not None:
                        sp.wait_ge(row_free, turn * GROUP + j + 1)
                    for k in range(2):
                        sp.dma_start(row[j][k][:, 0:FEAT], xn_d[at(first[j], P), :]).then_inc(row_in[j], 16)

            def load_xnew(tile):
                sp.dma_start(xnew[:], xnew_d.rearrange("(t p) f -> p t f", p=P)[:, at(tile, GROUP), :]
                             ).then_inc(xnew_in, 16)

            def store(tile):
                sp.dma_start(out[0:NPAD, :].rearrange("(t p) f -> p t f", p=P)[:, at(tile, GROUP), :], ob[:]
                             ).then_inc(o_out, 16)

            def load_columns(h, col):
                sp.wait_ge(up_done, (h + 1) * UP)
                for i, part in enumerate((xhi, xlo)):
                    sp.dma_start(part[:].bitcast(F32), xT_d[i, :, :, at(col, SH)]).then_inc(xT_in, 16)

            sp.dma_start(b2_sb[:], v["b2"].rearrange("(o e) f -> o e f", o=1).to_broadcast([P, EXPERTS + 1, FEAT])
                         ).then_inc(b_in, 16)
            load_xnew((NG - 1) * GROUP)
            load_rows(None, NG - 1)
            load_weights(sp, raw, w1, w2, 1, w_in)
            sp.sem_inc(ob_free, 1)
            load_columns(0, 0)
            sp.wait_ge(ob_done, GROUP + 1)
            store((NG - 1) * GROUP)
            load_xnew(0)
            sp.wait_ge(o_out, 16)
            sp.sem_inc(ob_free, 1)
            load_rows(1, 0)
            with sp.Fori(1, NG - 1) as h:
                col = sp.snap(h * SH)
                tile = sp.snap(h * GROUP)
                before = sp.snap((h - 1) * GROUP)
                load_columns(h, col)
                load_rows(h + 1, h)
                sp.wait_ge(ob_done, (h + 1) * GROUP + 1)
                store(before)
                load_xnew(tile)
                sp.wait_ge(o_out, (h + 1) * 16)
                sp.sem_inc(ob_free, 1)
            sp.wait_ge(row_free, NT + GROUP)
            sp.dma_start(v["slot_tile"][:], slots_d[0:TOK, :].rearrange("(m p) f -> p m f", p=P)
                         ).then_inc(v["slot_in"], 16)
            sp.wait_ge(wlo_done, 2)
            load_weights(sp, raw, w1, w2, 2, w_in)
            sp.wait_ge(ob_done, NT + 1)
            store((NG - 2) * GROUP)

        @block.gpsimd
        def _(pool):
            pool.iota(falling[:], [[-1, EXPERTS]], base=EXPERTS, channel_multiplier=0,
                      allow_small_or_imprecise_dtypes=True)
            pool.iota(token_i[:], [[P, NT]], base=0, channel_multiplier=1).then_inc(r_consts, 1)
            pool.sem_inc(row_free, GROUP)
            pool.wait_ge(placed, 1)

            def send(g, group):
                for j in range(GROUP):
                    t = group * GROUP + j
                    pool.wait_ge(row_free, g * GROUP + GROUP)
                    pool.tensor_copy(pos_st[j][:], pos_i[:, at(t), :].rearrange("p o k -> p (o k)"))
                    for k in range(2):
                        ins = pool.tensor_copy(row[j][k][:, FEAT:ROW].bitcast(I32),
                                               meta_i[:, at(t), k, :].rearrange("p o m -> p (o m)"))
                    ins.then_inc(pos_staged, 1)
                for j in range(GROUP):
                    pool.wait_ge(pos_staged, g * GROUP + j + 1)
                    pool.wait_ge(row_in[j], 32 * (g + 1))
                    pool.sem_inc(row_go, 1)
                    for k in range(2):
                        pool.indirect_dma_start(
                            out=slots_d, out_offset=bass.IndirectOffsetOnAxis(ap=pos_st[j][:, k:k + 1], axis=0),
                            in_=row[j][k][:], in_offset=None).then_inc(sent[j], 16)
                for j in range(GROUP):
                    pool.wait_ge(sent[j], 32 * (g + 1))
                    pool.sem_inc(row_free, 1)

            send(0, NG - 1)
            with pool.Fori(0, NG - 1) as h:
                send(h + 1, h)

        @block.scalar
        def _(act):
            act.sem_inc(gelu_done, 4)
            nc.scalar.activation(warm[:, 0:1], v["ones"][:, 0:1], ACT.Exp)
            act.wait_ge(shift_done, 1)
            nc.scalar.activation(expd[:], shifted[:], ACT.Exp).then_inc(exp_done, 1)
            nc.scalar.activation(warm[:, 1:2], v["ones"][:, 0:1], ACT.Gelu)

            def hidden(g):
                def high(i):
                    f, half = i // 2, i % 2
                    act.wait_ge(gelu_done, g * UP + i + 1 + 4)
                    if i == 0:
                        act.wait_ge(down_done, g * GROUP + GROUP)
                    nc.scalar.activation(hhi[:, f, SHH * half:SHH * half + SHH], hf[i % 4][:], ACT.Copy
                                         ).then_inc(hhi_done, 1)

                for i in range(UP):
                    act.wait_ge(up_done, g * UP + i + 1)
                    act.wait_ge(hlo_done, g * UP + i + 1)
                    nc.scalar.activation(hf[i % 4][:], psA[i % 4][:, 0:SHH], ACT.Gelu, bias=b1_sb[:, 0, i // 2:i // 2 + 1]
                                         ).then_inc(gelu_done, 1)
                    if i > 0:
                        high(i - 1)
                high(UP - 1)

            with act.Fori(0, NG - 1) as h:
                hidden(h)
                act.wait_ge(w_in, 64)
                part = at(h * WP, WP)
                nc.scalar.activation(whi[1][:, part], raw[:, part], ACT.Copy).then_inc(whi_part, 1)
            hidden(NG - 1)
            act.wait_ge(whi_part, NG - 1)
            act.sem_inc(whi_done, 1)

        @block.vector
        def _(dve):
            link = chain_of(dve, r_step)
            (shift, softmax, best_value, best_expert, choose, gates, counts, doubling, tiles_needed, first_tiles,
             slots, place, DOUBLINGS) = route_steps(nc, router, sb, dve, link, psR, psT)

            def low(g, i):
                f, half = i // 2, i % 2
                cols = slice(SHH * half, SHH * half + SHH)
                dve.wait_ge(hhi_done, g * UP + i + 1)
                nc.vector.tensor_tensor(hlo[:, f, cols], hf[i % 4][:], hhi[:, f, cols].bitcast(F32),
                                        ALU.subtract).then_inc(hlo_done, 1)

            def rows_ready(g):
                dve.wait_ge(xnew_in, 16 * (g + 1))
                if isinstance(g, int):
                    dve.wait_ge(b_in, 16)
                dve.wait_ge(ob_free, g + 1)

            def output(g, j):
                t = g * GROUP + j
                dve.wait_ge(down_done, t + 1 + GROUP)
                nc.vector.tensor_tensor(biased[:, j % 2, :], psB[j % 2][:, 0:FEAT], b2_sb[:, 0, :], ALU.add
                                        ).then_inc(biased_done, 1)
                dve.wait_ge(biased_done, t + 1)
                nc.vector.tensor_tensor(ob[:, j, :], biased[:, j % 2, :], xnew[:, j, :], ALU.add
                                        ).then_inc(ob_done, 1)

            shift()
            dve.sem_inc(hlo_done, 4)
            dve.sem_inc(ob_done, 1)
            for i in range(UP):
                if i == 0:
                    dve.wait_ge(r_consts, 1)
                    softmax()
                    best_value(0)
                low(0, i)
                if i == 2:
                    best_expert(0)
                if i == 5:
                    best_value(1)
                if i == 8:
                    best_expert(1)
                if i == 11:
                    choose()
                if i == 14:
                    gates()
            rows_ready(0)
            for j in range(GROUP):
                if j == 0:
                    counts()
                if j == 1:
                    for n in range(0, 2):
                        doubling(n)
                if j == 2:
                    for n in range(2, DOUBLINGS):
                        doubling(n)
                if j == 3:
                    tiles_needed()
                    first_tiles()
                if j == 4:
                    slots()
                output(0, j)
            place()
            with dve.Fori(0, NG - 1) as h:
                g = h + 1
                for i in range(UP):
                    low(g, i)
                rows_ready(g)
                output(g, 0)
                dve.wait_ge(whi_part, h + 1)
                part = at(h * WP, WP)
                nc.vector.tensor_tensor(wlo[1][:, part], raw[:, part], whi[1][:, part].bitcast(F32), ALU.subtract
                                        ).then_inc(wlo_part, 1)
                for j in range(1, GROUP):
                    output(g, j)
            dve.wait_ge(wlo_part, NG - 1)
            dve.sem_inc(wlo_done, 1)

        @block.tensor
        def _(pe):
            pe.sem_inc(down_done, GROUP)

            def up(g, i):
                f, half = i // 2, i % 2
                pe.wait_ge(gelu_done, g * UP + i + 1)
                up_product(nc, psA[i % 4][:, 0:SHH], whi[0], wlo[0],
                           lambda k, half=half: xhi[:, k, SHH * half:SHH * half + SHH],
                           lambda k, half=half: xlo[:, k, SHH * half:SHH * half + SHH], f).then_inc(up_done, 1)

            def down(g, j):
                t = g * GROUP + j
                pe.wait_ge(ob_done, t + 1 if j == 0 else t)
                for f in range(FC):
                    if j == 0:
                        pe.wait_ge(hlo_done, g * UP + 2 * f + 2 + 4)
                    ins = down_product(nc, psB[j % 2][:, 0:FEAT], hhi[:, f, P * j:P * j + P],
                                       hlo[:, f, P * j:P * j + P], whi[0], wlo[0], f)
                ins.then_inc(down_done, 1)

            def count():
                pe.wait_ge(chosen_done, 1)
                flat = chosen[:].rearrange("p t e -> p (t e)")
                nc.tensor.matmul(psR[:, 0:NT * EXPERTS], v["earlier"][:], flat, start=True, stop=True)
                nc.tensor.matmul(psT[:, 0:NT * EXPERTS], v["ones"][:], flat, start=True, stop=True).then_inc(counted, 1)

            for i in range(UP):
                up(0, i)
            count()
            for j in range(GROUP):
                down(0, j)
            with pe.Fori(0, NG - 1) as h:
                g = h + 1
                pe.wait_ge(xT_in, 32 * g)
                for i in range(UP):
                    up(g, i)
                for j in range(GROUP):
                    down(g, j)


def routed_block(nc, v):
    raw, whi, wlo, b1_sb, b2_sb = v["raw"], v["whi"], v["wlo"], v["b1_sb"], v["b2_sb"]
    w1, w2, out, slots_d, ident, counts_i = (v[k] for k in ("w1", "w2", "out", "slots_d", "ident", "counts_i"))

    with ExitStack() as ctx:
        def sb(name, shape, dt=F32):
            return ctx.enter_context(nc.sbuf_tensor(name, shape, dt))

        def pb(name):
            return ctx.enter_context(nc.psum_tensor(name, [P, 512], F32))

        def sem(name):
            return ctx.enter_context(nc.semaphore(name))

        rows = v["slot_tile"]
        meta = sb("q_meta", [P, SUB, 2], I32)
        index = [sb(f"q_index{m}", [P, 1], I32) for m in range(SUB)]
        xf = sb("q_xf", [P, KC, TOK])
        xhi = sb("q_xhi", [P, KC, TOK], F32R)
        xlo = sb("q_xlo", [P, KC, TOK], F32R)
        hf = [sb(f"q_hf{i}", [P, TOK]) for i in range(FC)]
        hhi = sb("q_hhi", [P, FC, TOK], F32R)
        hlo = sb("q_hlo", [P, FC, TOK], F32R)
        b1_st = sb("q_b1", [P, FC])
        b2_st = sb("q_b2", [P, FEAT])
        biased = sb("q_biased", [P, SUB, FEAT])
        ob = [sb(f"q_ob{m}", [P, FEAT]) for m in range(SUB)]
        psA = [pb(f"q_psA{i}") for i in range(4)]
        psB = [pb(f"q_psB{i}") for i in range(SUB)]
        psX = pb("q_psX")

        w_in, whi_done, wlo_done = v["w_in"], v["whi_done"], v["wlo_done"]
        rows_in, added, w_go = v["slot_in"], sem("q_added"), sem("q_w_go")
        add_go, ob_free, b1_done, b2_done = sem("q_add_go"), sem("q_ob_free"), sem("q_b1_done"), sem("q_b2_done")
        turned, xf_done = sem("q_turned"), sem("q_xf_done")
        begun = sem("q_begun")
        xhi_done, xlo_done, meta_done = sem("q_xhi_done"), sem("q_xlo_done"), sem("q_meta_done")
        up_done, gelu_done, hhi_done, hlo_done = sem("q_up_done"), sem("q_gelu_done"), sem("q_hhi_done"), sem("q_hlo_done")
        down_done, biased_done, ob_done = sem("q_down_done"), sem("q_biased_done"), sem("q_ob_done")
        block = ctx.enter_context(nc.Block())


        def experts(eng, expert):
            def one(e, h):
                n = eng.value_load(counts_i[0:1, at(e)], min_val=LEAST, max_val=TILES)
                first = eng.value_load(counts_i[0:1, at(e + EXPERTS)], min_val=0, max_val=TILES - LEAST)
                expert(e, h, n, first)

            with eng.Fori(0, EXPERTS // 2 - 1) as pair:
                one(pair * 2, 0)
                one(pair * 2 + 1, 1)
            one(EXPERTS - 2, 0)
            one(EXPERTS - 1, 1)

        def further(eng, n, first, tile):
            with eng.Fori(2, n) as i:
                tile(nc.s_assert_within(first + i, 0, TILES - 1, skip_runtime_bounds_check_because=
                                        "the experts' tiles add up to TILES at most"))

        def second(first):
            return nc.s_assert_within(first + 1, 0, TILES - 1, skip_runtime_bounds_check_because=
                                      "every expert has its first two tiles")

        def splits_next(e):
            return not (isinstance(e, int) and e == EXPERTS - 1)

        def piece(w, n):
            width = (KC * HID + FC * FEAT) // PIECES
            return w[:, n * width:(n + 1) * width]


        @block.sync
        def _(sp):
            def load_rows(s):
                first_row = sp.snap((s + 1) * TOK)
                sp.wait_ge(meta_done, s + 1)
                sp.dma_start(rows[:], slots_d[at(first_row, TOK), :].rearrange("(m p) f -> p m f", p=P)
                             ).then_inc(rows_in, 16)

            def expert(e, h, n, first):
                load_rows(first)
                load_rows(second(first))
                if not isinstance(e, int):
                    sp.wait_ge(wlo_done, (e + 1) * PIECES + 2)
                    sp.sem_inc(w_go, 1)
                    load_weights(sp, raw, w1, w2, e + 3, w_in)
                further(sp, n, first, load_rows)

            experts(sp, expert)

        @block.gpsimd
        def _(pool):
            pool.sem_inc(ob_free, SUB)
            pool.wait_ge(v["o_out"], 16 * NG)

            def tile(s):
                for m in range(SUB):
                    pool.wait_ge(ob_done, s * SUB + m + 1 + SUB)
                    pool.sem_inc(add_go, 1)
                    pool.indirect_dma_start(
                        out=out, out_offset=bass.IndirectOffsetOnAxis(ap=index[m][:], axis=0),
                        in_=ob[m][:], in_offset=None, compute_op=ALU.add).then_inc(added, 16)
                    pool.wait_ge(added, (s * SUB + m + 1) * 16)
                    pool.sem_inc(ob_free, 1)

            def expert(e, h, n, first):
                tile(first)
                tile(second(first))
                further(pool, n, first, tile)

            experts(pool, expert)

        @block.scalar
        def _(act):
            act.sem_inc(gelu_done, 4)
            act.wait_ge(turned, 1)
            nc.scalar.activation(xf[:].rearrange("p k n -> p (k n)"), psX[:], ACT.Copy).then_inc(xf_done, 1)

            def tile(s, after=None, pieces=0):
                for f in range(FC):
                    act.wait_ge(up_done, s * FC + f + 1)
                    act.wait_ge(hlo_done, s * FC + f + 1)
                    nc.scalar.activation(hf[f][:], psA[f % 4][:, 0:TOK], ACT.Gelu, bias=b1_st[:, f:f + 1]
                                         ).then_inc(gelu_done, 1)
                    if after is not None and f % 2 == 1:
                        after(pieces + f // 2)
                act.wait_ge(turned, s + 2)
                act.wait_ge(xlo_done, s + 1)
                nc.scalar.activation(xf[:].rearrange("p k n -> p (k n)"), psX[:], ACT.Copy).then_inc(xf_done, 1)

            def expert(e, h, n, first):
                act.wait_ge(gelu_done, first * FC + 4)
                nc.scalar.activation(b1_st[:], b1_sb[:, at(e + 1), :].rearrange("p o f -> p (o f)"), ACT.Copy
                                     ).then_inc(b1_done, 1)
                act.wait_ge(b1_done, e + 1)

                def split(f):
                    if f == 0:
                        act.wait_ge(down_done, first * SUB + SUB)
                        act.wait_ge(w_in, e * 32 + 32 * 3)
                    nc.scalar.activation(piece(whi[h], f), piece(raw, f), ACT.Copy).then_inc(whi_done, 1)

                tile(first, split if splits_next(e) else None, 0)
                tile(second(first), split if splits_next(e) else None, PIECES // 2)
                act.sem_inc(begun, 1)
                further(act, n, first, tile)

            experts(act, expert)

        @block.vector
        def _(dve):
            dve.sem_inc(hlo_done, FC)
            dve.sem_inc(ob_done, SUB)

            def split_x(s):
                dve.wait_ge(xf_done, s + 1)
                nc.vector.tensor_copy(xhi[:], xf[:]).then_inc(xhi_done, 1)
                dve.wait_ge(xhi_done, s + 1)
                nc.vector.tensor_tensor(xlo[:], xf[:], xhi[:].bitcast(F32), ALU.subtract).then_inc(xlo_done, 1)

            split_x(0)
            nc.vector.tensor_copy(meta[:], rows[:, :, FEAT:ROW].bitcast(I32)).then_inc(meta_done, 1)

            def high(s, f):
                dve.wait_ge(gelu_done, s * FC + f + 1 + 4)
                nc.vector.tensor_copy(hhi[:, f, :], hf[f][:]).then_inc(hhi_done, 1)

            def low(s, f):
                dve.wait_ge(hhi_done, s * FC + f + 1)
                nc.vector.tensor_tensor(hlo[:, f, :], hf[f][:], hhi[:, f, :].bitcast(F32), ALU.subtract
                                        ).then_inc(hlo_done, 1)

            def tile(s, after=None, pieces=0):
                dve.wait_ge(down_done, s * SUB + SUB)
                high(s, 0)
                for f in range(FC):
                    if f + 1 < FC:
                        high(s, f + 1)
                    low(s, f)
                    if after is not None and f % 2 == 1:
                        after(pieces + f // 2)
                split_x(s + 1)
                dve.wait_ge(ob_free, s * SUB + SUB)
                for m in range(SUB):
                    dve.wait_ge(down_done, s * SUB + m + 1 + SUB)
                    nc.vector.tensor_copy(index[m][:], meta[:, m, 0:1])
                    nc.vector.tensor_tensor(biased[:, m, :], psB[m][:, 0:FEAT], b2_st[:], ALU.add
                                            ).then_inc(biased_done, 1)
                    dve.wait_ge(biased_done, s * SUB + m + 1)
                    nc.vector.tensor_scalar(ob[m][:], biased[:, m, :], meta[:, m, 1:2].bitcast(F32), None, ALU.mult
                                            ).then_inc(ob_done, 1)
                dve.wait_ge(ob_done, s * SUB + SUB + SUB)
                nc.vector.tensor_copy(meta[:], rows[:, :, FEAT:ROW].bitcast(I32)).then_inc(meta_done, 1)

            def expert(e, h, n, first):
                dve.wait_ge(ob_done, first * SUB + SUB)
                nc.vector.tensor_copy(b2_st[:], b2_sb[:, at(e + 1), :].rearrange("p o f -> p (o f)")
                                      ).then_inc(b2_done, 1)
                dve.wait_ge(b2_done, e + 1)

                def split(f):
                    dve.wait_ge(whi_done, e * PIECES + f + 1 + 2)
                    nc.vector.tensor_tensor(piece(wlo[h], f), piece(raw, f), piece(whi[h], f).bitcast(F32),
                                            ALU.subtract).then_inc(wlo_done, 1)

                tile(first, split if splits_next(e) else None, 0)
                tile(second(first), split if splits_next(e) else None, PIECES // 2)
                dve.sem_inc(begun, 1)
                further(dve, n, first, tile)

            experts(dve, expert)

        @block.tensor
        def _(pe):
            pe.sem_inc(down_done, SUB)

            def turn(s):
                pe.wait_ge(rows_in, (s + 1) * 16)
                for k in range(KC):
                    for m in range(SUB):
                        ins = nc.tensor.transpose(psX[:, TOK * k + P * m:TOK * k + P * m + P],
                                                  rows[:, m, P * k:P * k + P], ident[:])
                ins.then_inc(turned, 1)

            turn(0)

            def expert(e, h, n, first):
                pe.wait_ge(wlo_done, e * PIECES + 2)
                pe.sem_inc(begun, 1)
                tile(first, h)
                tile(second(first), h)
                further(pe, n, first, lambda s: tile(s, h))

            def tile(s, h):
                hi, lo = whi[1 - h], wlo[1 - h]
                pe.wait_ge(xlo_done, s + 1)
                for f in range(FC):
                    pe.wait_ge(gelu_done, s * FC + f + 1)
                    up_product(nc, psA[f % 4][:, 0:TOK], hi, lo, lambda k: xhi[:, k, :], lambda k: xlo[:, k, :], f
                               ).then_inc(up_done, 1)
                for f in range(FC):
                    pe.wait_ge(hlo_done, s * FC + f + 1 + FC)
                    if f == 0:
                        pe.wait_ge(ob_done, s * SUB + SUB)
                    if f == FC // 2:
                        pe.wait_ge(xf_done, s + 1)
                        turn(s + 1)
                    for m in range(SUB):
                        ins = down_product(nc, psB[m][:, 0:FEAT], hhi[:, f, P * m:P * m + P],
                                           hlo[:, f, P * m:P * m + P], hi, lo, f)
                        if f == FC - 1:
                            ins.then_inc(down_done, 1)

            experts(pe, expert)


def kernel(**inputs):
    import concourse.bacc as bacc
    from concourse.bass_utils import run_bass_kernel_spmd

    a = {k: np.asarray(v) for k, v in inputs.items()}

    def rows(m, n, mode="constant"):
        return np.pad(m, [(0, n - m.shape[0])] + [(0, 0)] * (m.ndim - 1), mode=mode)

    src = rows(a["src"], EPAD, "edge").reshape(T * C, P).T
    dst = rows(a["dst"], EPAD, "edge")
    sh = rows(a["edge_attr_4"], EPAD).reshape(T, C, P, 4).transpose(2, 0, 1, 3).reshape(P, T * C * 4)
    fc1 = a["L0_gnn_fc_w1"]
    columns = [fc1[:, MUL * k:MUL * (k + 1)] for k in (1, 0, 3, 2)]
    b1 = np.concatenate([a["L0_ffn_b1s"][None], a["L0_ffn_b1p"]]).reshape(EXPERTS + 1, FC, P).transpose(2, 0, 1)
    arrays = {
        "x": rows(a["x"], NPAD),
        "src_t": src,
        "dst_t": dst.reshape(T * C, P).T,
        "dst_w": dst.reshape(T, STEP),
        "sh_t": sh,
        "ele_t": rows(a["edge_attr_8"], EPAD).T,
        "z_t": rows(a["node_vec1"], NPAD).reshape(NT, P).T,
        "w_sc0": a["L0_gnn_W_sc0"],
        "w_sc1": a["L0_gnn_W_sc1"],
        "w_l0": a["L0_gnn_W_lin1_0"],
        "w_l1": a["L0_gnn_W_lin1_1"],
        "fc0": np.tile(a["L0_gnn_fc_w0"], (2, 2)),
        "fc1": np.tile(np.concatenate(columns, axis=1), (2, 1)),
        "w_20": a["L0_gnn_W_lin2_0"],
        "w_21": a["L0_gnn_W_lin2_1"],
        "w_r": a["L0_ffn_Wr"],
        "w1": np.concatenate([a["L0_ffn_W1s"][None], a["L0_ffn_W1p"]]),
        "b1": b1.reshape(P, (EXPERTS + 1) * FC),
        "w2": np.concatenate([a["L0_ffn_W2s"][None], a["L0_ffn_W2p"]]),
        "b2": np.concatenate([a["L0_ffn_b2s"][None], a["L0_ffn_b2p"]]),
    }
    nc = bacc.Bacc("TRN2", target_bir_lowering=False, num_devices=1)
    given, args = {}, {}
    for name, m in arrays.items():
        m = np.ascontiguousarray(m)
        given[f"in_{name}"] = m
        args[name] = nc.dram_tensor(f"in_{name}", m.shape, mybir.dt.from_np(m.dtype), kind="ExternalInput").ap()
    args["out"] = nc.dram_tensor("out_rows", (NPAD + P, FEAT), F32, kind="ExternalOutput").ap()
    gnn_moe_kernel(nc, **args)
    result = run_bass_kernel_spmd(nc, [given], core_ids=[0]).results[0]["out_rows"]
    return result[:NODES]
```
